# Optimizing a Trainium2 kernel written in Bass

```python
import numpy as np
import jax
import jax.numpy as jnp

def _softmax(x, axis=-1):
    return jax.nn.softmax(x, axis=axis)

def _gelu(x):
    return jax.nn.gelu(x, approximate=True)

def _silu(x):
    return jax.nn.silu(x)

def _sigmoid(x):
    return jax.nn.sigmoid(x)

def _layernorm(x, axis=-1, eps=1e-05):
    m = jnp.mean(x, axis=axis, keepdims=True)
    v = jnp.var(x, axis=axis, keepdims=True)
    return (x - m) / jnp.sqrt(v + eps)

def _scatter_add(tgt, idx, src, axis=0):
    return tgt.at[idx].add(src)

def _segment_sum(src, seg, n):
    return jax.ops.segment_sum(src, seg, n)
kernel_name = 'mk_hybrid_d1_jaxref_r4_fbbbec'

def setup_inputs(seed: int=0):
    np.random.seed(seed)
    _w = jnp.asarray

    def _L0_attn_a_setup():
        import jax, jax.numpy as jnp
        import numpy as np
        B, S, D_IN = (2, 512, 256)
        H, D_HEAD = (16, 64)
        key = jax.random.key(seed)
        k1, k2, k3 = jax.random.split(key, 3)
        x = jax.random.normal(k1, (B, S, D_IN), dtype=jnp.float32)
        kernel = jax.random.normal(k2, (3, H, D_IN, D_HEAD), dtype=jnp.float32) * np.float32(np.sqrt(2.0 / D_IN))
        WO = jax.random.normal(k3, (1, H * D_HEAD, D_IN), dtype=jnp.float32) * np.float32(np.sqrt(2.0 / (H * D_HEAD)))
        return {'x': x, 'kernel': kernel, 'WO': WO}
    _L0_attn_a_in = _L0_attn_a_setup()

    def _L0_attn_b_setup():
        import jax, jax.numpy as jnp
        import numpy as np
        B, S, D = (2, 512, 256)
        H, DH = (16, 64)
        DQL, DKVL = (128, 128)
        DR = 64
        TOPK = 64
        LN_EPS = 1e-05
        ROPE_BASE = 10000.0

        def _rope_tables(seq_len, dim):
            inv_freq = 1.0 / ROPE_BASE ** (np.arange(0, dim, 2, dtype=np.float32) / dim)
            t = np.arange(seq_len, dtype=np.float32)
            freqs = np.outer(t, inv_freq)
            cos = np.concatenate([np.cos(freqs), np.cos(freqs)], -1)[:, ::2]
            sin = np.concatenate([np.sin(freqs), np.sin(freqs)], -1)[:, ::2]
            return (jnp.asarray(cos), jnp.asarray(sin))

        def _apply_rope_subspace(x, d_rope):
            s = x.shape[-2]
            cos, sin = _rope_tables(s, d_rope)
            xr, xp = (x[..., :d_rope], x[..., d_rope:])
            e, o = (xr[..., 0::2], xr[..., 1::2])
            rot = jnp.stack([e * cos - o * sin, e * sin + o * cos], axis=-1).reshape(xr.shape)
            return jnp.concatenate([rot, xp], axis=-1)

        def _reference_tuple_inner(x, w_down_q, w_down_kv, w_up_q, w_up_k, w_up_v, w_out, ln_scale, ln_bias):
            b, s, d = x.shape
            residual = x
            mu = jnp.mean(x, axis=-1, keepdims=True)
            var = jnp.mean((x - mu) ** 2, axis=-1, keepdims=True)
            h = (x - mu) * jax.lax.rsqrt(var + LN_EPS) * ln_scale + ln_bias
            c_q = h @ w_down_q.T
            c_kv = h @ w_down_kv.T
            q = (c_q @ w_up_q.T).reshape(b, s, H, DH).transpose(0, 2, 1, 3)
            k = (c_kv @ w_up_k.T).reshape(b, s, H, DH).transpose(0, 2, 1, 3)
            v = (c_kv @ w_up_v.T).reshape(b, s, H, DH).transpose(0, 2, 1, 3)
            q = _apply_rope_subspace(q, DR)
            k = _apply_rope_subspace(k, DR)
            scale = 1.0 / np.sqrt(DH).astype(np.float32)
            scores = jnp.einsum('bhqd,bhkd->bhqk', q, k) * scale
            _, indices = jax.lax.top_k(scores, min(TOPK, s))
            attn = jax.nn.softmax(scores, axis=-1)
            out = jnp.einsum('bhqk,bhkd->bhqd', attn, v)
            out = out.transpose(0, 2, 1, 3).reshape(b, s, H * DH)
            out = out @ w_out.T + residual
            return (out, indices.astype(jnp.int64))
        key = jax.random.key(seed)
        ks = jax.random.split(key, 7)
        init = lambda k, shape: jax.random.normal(k, shape, jnp.float32) * 0.02
        return {'x': jax.random.normal(ks[0], (B, S, D), jnp.float32), 'w_down_q': init(ks[1], (DQL, D)), 'w_down_kv': init(ks[2], (DKVL, D)), 'w_up_q': init(ks[3], (H * DH, DQL)), 'w_up_k': init(ks[4], (H * DH, DKVL)), 'w_up_v': init(ks[5], (H * DH, DKVL)), 'w_out': init(ks[6], (D, H * DH)), 'ln_scale': jnp.ones((D,), jnp.float32), 'ln_bias': jnp.zeros((D,), jnp.float32)}
    _L0_attn_b_in = _L0_attn_b_setup()

    def _L0_ffn_setup():
        import jax, jax.numpy as jnp
        import numpy as np
        N_EMBD = 256
        N_STATE = 1024
        key = jax.random.key(seed)
        k_x, k_w1, k_b1, k_w2, k_b2 = jax.random.split(key, 5)
        x = jax.random.normal(k_x, (4, 512, N_EMBD), dtype=jnp.float32)
        w1 = jax.random.normal(k_w1, (N_EMBD, N_STATE), dtype=jnp.float32) * (1.0 / np.sqrt(N_EMBD))
        b1 = jax.random.normal(k_b1, (N_STATE,), dtype=jnp.float32) * 0.02
        w2 = jax.random.normal(k_w2, (N_STATE, N_EMBD), dtype=jnp.float32) * (1.0 / np.sqrt(N_STATE))
        b2 = jax.random.normal(k_b2, (N_EMBD,), dtype=jnp.float32) * 0.02
        return {'x': x, 'w1': w1, 'b1': b1, 'w2': w2, 'b2': b2}
    _L0_ffn_in = _L0_ffn_setup()
    _d = {'L0_attn_a_x': _L0_attn_a_in['x'], 'L0_attn_a_kernel': _L0_attn_a_in['kernel'], 'L0_attn_a_WO': _L0_attn_a_in['WO'], 'L0_attn_b_w_down_q': _L0_attn_b_in['w_down_q'], 'L0_attn_b_w_down_kv': _L0_attn_b_in['w_down_kv'], 'L0_attn_b_w_up_q': _L0_attn_b_in['w_up_q'], 'L0_attn_b_w_up_k': _L0_attn_b_in['w_up_k'], 'L0_attn_b_w_up_v': _L0_attn_b_in['w_up_v'], 'L0_attn_b_w_out': _L0_attn_b_in['w_out'], 'L0_attn_b_ln_scale': _L0_attn_b_in['ln_scale'], 'L0_attn_b_ln_bias': _L0_attn_b_in['ln_bias'], 'L0_ffn_w1': _L0_ffn_in['w1'], 'L0_ffn_b1': _L0_ffn_in['b1'], 'L0_ffn_w2': _L0_ffn_in['w2'], 'L0_ffn_b2': _L0_ffn_in['b2']}
    _x0 = _d['L0_attn_a_x']
    _d['L0_attn_a_x'] = jax.random.normal(jax.random.fold_in(jax.random.key(seed), 1), (4, 1024, 256), dtype=_x0.dtype)
    del _x0
    return _d

def reference(L0_attn_a_x, L0_attn_a_kernel, L0_attn_a_WO, L0_attn_b_w_down_q, L0_attn_b_w_down_kv, L0_attn_b_w_up_q, L0_attn_b_w_up_k, L0_attn_b_w_up_v, L0_attn_b_w_out, L0_attn_b_ln_scale, L0_attn_b_ln_bias, L0_ffn_w1, L0_ffn_b1, L0_ffn_w2, L0_ffn_b2):

    def _L0_attn_a_ref(x, kernel, WO):
        import jax, jax.numpy as jnp
        import numpy as np
        B, S, D_IN = (2, 512, 256)
        H, D_HEAD = (16, 64)
        b, s, _ = x.shape
        h, d = (kernel.shape[1], kernel.shape[3])
        q = jnp.einsum('bsm,hmd->bhsd', x, kernel[0])
        k = jnp.einsum('bsm,hmd->bhsd', x, kernel[1])
        v = jnp.einsum('bsm,hmd->bhsd', x, kernel[2])
        scale = jnp.float32(1.0 / (d * d * h))
        scores = jnp.einsum('bhsd,bhtd->bhst', q, k) * scale
        attn = jax.nn.softmax(scores, axis=-1)
        out = jnp.einsum('bhst,bhtd->bhsd', attn, v)
        out = jnp.transpose(out, (0, 2, 3, 1)).reshape(b, s, d * h)
        out = jnp.einsum('bsf,fm->bsm', out, WO[0])
        return out

    def _L0_attn_b_ref(x, w_down_q, w_down_kv, w_up_q, w_up_k, w_up_v, w_out, ln_scale, ln_bias):
        import jax, jax.numpy as jnp
        import numpy as np
        B, S, D = (2, 512, 256)
        H, DH = (16, 64)
        DQL, DKVL = (128, 128)
        DR = 64
        TOPK = 64
        LN_EPS = 1e-05
        ROPE_BASE = 10000.0

        def _rope_tables(seq_len, dim):
            inv_freq = 1.0 / ROPE_BASE ** (np.arange(0, dim, 2, dtype=np.float32) / dim)
            t = np.arange(seq_len, dtype=np.float32)
            freqs = np.outer(t, inv_freq)
            cos = np.concatenate([np.cos(freqs), np.cos(freqs)], -1)[:, ::2]
            sin = np.concatenate([np.sin(freqs), np.sin(freqs)], -1)[:, ::2]
            return (jnp.asarray(cos), jnp.asarray(sin))

        def _apply_rope_subspace(x, d_rope):
            s = x.shape[-2]
            cos, sin = _rope_tables(s, d_rope)
            xr, xp = (x[..., :d_rope], x[..., d_rope:])
            e, o = (xr[..., 0::2], xr[..., 1::2])
            rot = jnp.stack([e * cos - o * sin, e * sin + o * cos], axis=-1).reshape(xr.shape)
            return jnp.concatenate([rot, xp], axis=-1)

        def _reference_tuple_inner(x, w_down_q, w_down_kv, w_up_q, w_up_k, w_up_v, w_out, ln_scale, ln_bias):
            b, s, d = x.shape
            residual = x
            mu = jnp.mean(x, axis=-1, keepdims=True)
            var = jnp.mean((x - mu) ** 2, axis=-1, keepdims=True)
            h = (x - mu) * jax.lax.rsqrt(var + LN_EPS) * ln_scale + ln_bias
            c_q = h @ w_down_q.T
            c_kv = h @ w_down_kv.T
            q = (c_q @ w_up_q.T).reshape(b, s, H, DH).transpose(0, 2, 1, 3)
            k = (c_kv @ w_up_k.T).reshape(b, s, H, DH).transpose(0, 2, 1, 3)
            v = (c_kv @ w_up_v.T).reshape(b, s, H, DH).transpose(0, 2, 1, 3)
            q = _apply_rope_subspace(q, DR)
            k = _apply_rope_subspace(k, DR)
            scale = 1.0 / np.sqrt(DH).astype(np.float32)
            scores = jnp.einsum('bhqd,bhkd->bhqk', q, k) * scale
            _, indices = jax.lax.top_k(scores, min(TOPK, s))
            attn = jax.nn.softmax(scores, axis=-1)
            out = jnp.einsum('bhqk,bhkd->bhqd', attn, v)
            out = out.transpose(0, 2, 1, 3).reshape(b, s, H * DH)
            out = out @ w_out.T + residual
            return (out, indices.astype(jnp.int64))
        return _reference_tuple_inner(x, w_down_q, w_down_kv, w_up_q, w_up_k, w_up_v, w_out, ln_scale, ln_bias)[0]

    def _L0_ffn_ref(x, w1, b1, w2, b2):
        import jax, jax.numpy as jnp
        import numpy as np
        N_EMBD = 256
        N_STATE = 1024
        h = jax.nn.gelu(jnp.einsum('bse,eh->bsh', x, w1) + b1, approximate=False)
        return jnp.einsum('bsh,he->bse', h, w2) + b2
    x = L0_attn_a_x
    x = x + _L0_attn_a_ref(_layernorm(x, axis=-1), L0_attn_a_kernel, L0_attn_a_WO)
    x = x + _L0_ffn_ref(_layernorm(x, axis=-1), L0_ffn_w1, L0_ffn_b1, L0_ffn_w2, L0_ffn_b2)
    x = x + _L0_attn_b_ref(_layernorm(x, axis=-1), L0_attn_b_w_down_q, L0_attn_b_w_down_kv, L0_attn_b_w_up_q, L0_attn_b_w_up_k, L0_attn_b_w_up_v, L0_attn_b_w_out, L0_attn_b_ln_scale, L0_attn_b_ln_bias)
    x = x + _L0_ffn_ref(_layernorm(x, axis=-1), L0_ffn_w1, L0_ffn_b1, L0_ffn_w2, L0_ffn_b2)
    return x

_drawn_inputs = setup_inputs


def setup_inputs(seed=0):
    import zlib

    import numpy as np

    out = dict(_drawn_inputs(seed))
    spreads = {'L0_attn_b_ln_scale': (1.0, 0.6), 'L0_attn_b_ln_bias': (0.0, 0.8)}
    factors = {'L0_attn_b_w_down_q': 8.0,
     'L0_attn_b_w_down_kv': 8.0,
     'L0_attn_b_w_up_q': 8.0,
     'L0_attn_b_w_up_k': 8.0,
     'L0_attn_b_w_up_v': 8.0,
     'L0_attn_b_w_out': 8.0,
     'L0_ffn_b1': 3.816}
    for name, (base, spread) in spreads.items():
        noise = np.random.default_rng([zlib.crc32(name.encode()), seed]).standard_normal(out[name].shape)
        drawn = base * np.exp(spread * noise) if base else spread * noise
        out[name] = jnp.asarray(drawn.astype(out[name].dtype))
    for name, factor in factors.items():
        out[name] = (out[name] * factor).astype(out[name].dtype)
    return out
```

```python
from contextlib import ExitStack

import numpy as np

import concourse.bass as bass
from concourse import mybir

F32 = mybir.dt.float32
F32R = mybir.dt.float32r
ACT = mybir.ActivationFunctionType
ALU = mybir.AluOpType
AX_X = mybir.AxisListType.X

P = 128
B, S, E = 4, 1024, 256
H, D = 16, 64
FF = 1024
TILES = B * S // P
BLOCK = 512
BLOCKS = B * S // BLOCK
BT = BLOCK // P
EC = E // P
FC = FF // P
KT = S // P
HALVES = S // BLOCK
EPS = 1e-5

PAIRS = H // 2
NPAIR = B * PAIRS
STEPS = 2 * KT
NSTEP = NPAIR * STEPS
GQ = 2
GW = GQ * P
GS = 2 * GQ
PG = STEPS // GS
NGROUP = NPAIR * PG
BODIES = NPAIR // 2
PRING = 4
NM = 4
T_LAG, PV_LAG, O_LAG, WO_LAG = 2, 6, 10, 12
assert B % 2 == 0 and PAIRS % 2 == 0 and PG == 4 and GS == 4


class Chain:

    def __init__(self, eng, sem):
        self.eng, self.sem, self.n = eng, sem, 0

    def __call__(self, ins):
        self.n += 1
        ins.then_inc(self.sem, 1)
        self.eng.wait_ge(self.sem, self.n)


def wait(eng, sem, value):
    if not isinstance(value, int) or value > 0:
        eng.wait_ge(sem, value)


def over_blocks(eng, body):
    body(0)
    with eng.Fori(1, BLOCKS) as k:
        body(k)


def tile_of(tensor, index, count=1):
    return tensor[:, bass.ds(index, count), :].rearrange("p a b -> p (a b)")


def pool_round(pool, hi, src, zero):
    return pool.tensor_tensor(hi, src, zero[:].to_broadcast(list(src.shape)), ALU.add)


def norm_tensors(nc, ctx, name):
    sb = lambda n, shape: ctx.enter_context(nc.sbuf_tensor(f"{name}_{n}", shape, F32))
    return {
        "stats": sb("stats", [P, TILES, 6]),
        "var": sb("var", [P, TILES]), "std": sb("std", [P, TILES]),
        "r": sb("r", [P, TILES]), "t": sb("t", [P, TILES]), "mean2": sb("mean2", [P, TILES]),
        "rstd": sb("rstd", [P, TILES]), "shift": sb("shift", [P, TILES]),
        "s_chain": ctx.enter_context(nc.semaphore(f"{name}_chain")),
        "s_var": ctx.enter_context(nc.semaphore(f"{name}_s_var")),
        "s_std": ctx.enter_context(nc.semaphore(f"{name}_s_std")),
        "s_done": ctx.enter_context(nc.semaphore(f"{name}_s_done")),
    }


def norm_vector(dve, N, src):
    with dve.Fori(0, TILES) as i:
        dve.bn_stats(tile_of(N["stats"], i), tile_of(src, i)).then_inc(N["s_done"], 1)
    dve.wait_ge(N["s_done"], TILES)
    st = N["stats"]
    me, mo, qe, qo = st[:, :, 1], st[:, :, 4], st[:, :, 2], st[:, :, 5]
    link = Chain(dve, N["s_chain"])
    link(dve.tensor_tensor(N["t"][:], me, mo, ALU.subtract))
    link(dve.tensor_tensor(N["mean2"][:], me, mo, ALU.add))
    link(dve.tensor_tensor(N["r"][:], N["t"][:], N["t"][:], ALU.mult))
    link(dve.tensor_tensor(N["t"][:], qe, qo, ALU.add))
    link(dve.scalar_tensor_tensor(N["var"][:], N["r"][:], E / 4.0, N["t"][:], ALU.mult, ALU.add))
    dve.tensor_scalar(N["t"][:], N["var"][:], 1.0 / E, EPS, ALU.mult, ALU.add).then_inc(N["s_var"], 1)
    dve.wait_ge(N["s_std"], 1)
    link(dve.reciprocal(N["r"][:], N["std"][:]))
    link(dve.tensor_tensor(N["std"][:], N["r"][:], N["r"][:], ALU.mult))
    link(dve.tensor_tensor(N["var"][:], N["std"][:], N["t"][:], ALU.mult))
    link(dve.tensor_scalar(N["std"][:], N["var"][:], -0.5, 1.5, ALU.mult, ALU.add))
    link(dve.tensor_tensor(N["rstd"][:], N["std"][:], N["r"][:], ALU.mult))
    link(dve.scalar_tensor_tensor(N["shift"][:], N["mean2"][:], -0.5, N["rstd"][:], ALU.mult, ALU.mult))


def norm_scalar(act, N):
    act.wait_ge(N["s_var"], 1)
    act.activation(N["std"][:], N["t"][:], ACT.Sqrt).then_inc(N["s_std"], 1)


def normalise(dve, dst, src, N, i):
    return dve.tensor_scalar(dst, src, N["rstd"][:, bass.ds(i, 1)], N["shift"][:, bass.ds(i, 1)],
                             ALU.mult, ALU.add)


def features_a(nc, x, ident, scratch):
    with ExitStack() as ctx:
        sb = lambda n, shape, dt=F32: ctx.enter_context(nc.sbuf_tensor(f"fa_{n}", shape, dt))
        sem = lambda n: ctx.enter_context(nc.semaphore(f"fa_{n}"))
        N = norm_tensors(nc, ctx, "fa_n")
        h = sb("h", [P, BT, E])
        hT = sb("hT", [P, 2 * EC, BLOCK], F32R)
        ps = ctx.enter_context(nc.psum_tensor("fa_ps", [P, EC, BLOCK], F32))
        s_h, s_t, s_split, s_out = sem("s_h"), sem("s_t"), sem("s_split"), sem("s_out")
        block = ctx.enter_context(nc.Block())

        @block.scalar
        def _(act):
            norm_scalar(act, N)

        @block.vector
        def _(dve):
            norm_vector(dve, N, x)
            def one_block(k):
                wait(dve, s_t, k * EC)
                for j in range(BT):
                    normalise(dve, h[:, j, :], tile_of(x, k * BT + j), N, k * BT + j).then_inc(s_h, 1)
                wait(dve, s_out, k * 16)
                for c in range(EC):
                    wait(dve, s_t, k * EC + c + 1)
                    dve.tensor_copy(hT[:, 2 * c, :], ps[:, c, :]).then_inc(s_split, 1)
                    wait(dve, s_split, k * 2 * EC + 2 * c + 1)
                    dve.tensor_tensor(hT[:, 2 * c + 1, :], ps[:, c, :], hT[:, 2 * c, :].bitcast(F32),
                                      ALU.subtract).then_inc(s_split, 1)
            over_blocks(dve, one_block)

        @block.tensor
        def _(pe):
            def one_block(k):
                wait(pe, s_h, (k + 1) * BT)
                wait(pe, s_split, k * 2 * EC)
                for c in range(EC):
                    for j in range(BT):
                        mm = pe.transpose(ps[:, c, j * P:(j + 1) * P], h[:, j, c * P:(c + 1) * P], ident[:])
                    mm.then_inc(s_t, 1)
            over_blocks(pe, one_block)

        @block.sync
        def _(sp):
            def one_block(k):
                wait(sp, s_split, (k + 1) * 2 * EC)
                sp.dma_start(scratch[k // HALVES, :, :, bass.ds((k % HALVES) * BLOCK, BLOCK)].bitcast(F32),
                             hT[:].bitcast(F32)).then_inc(s_out, 16)
            over_blocks(sp, one_block)
            sp.wait_ge(s_out, 16 * BLOCKS)


def features_b(nc, x, ident, zero, scratch, w_down, ln_affine):
    with ExitStack() as ctx:
        sb = lambda n, shape, dt=F32: ctx.enter_context(nc.sbuf_tensor(f"fb_{n}", shape, dt))
        sem = lambda n: ctx.enter_context(nc.semaphore(f"fb_{n}"))
        N1 = norm_tensors(nc, ctx, "fb_n1")
        N2 = norm_tensors(nc, ctx, "fb_n2")
        xn = sb("xn", [P, TILES, E])
        h = sb("h", [P, BT, E])
        hf = sb("hf", [P, EC, BLOCK])
        hT = sb("hT", [P, 2 * EC, BLOCK], F32R)
        cT = sb("cT", [P, 4, BLOCK], F32R)
        raw = sb("raw", [P, EC * 2 * P])
        wh = sb("wh", [P, EC, 2, P], F32R)
        wl = sb("wl", [P, EC, 2, P], F32R)
        affine = sb("affine", [P, 2 * EC])
        ps = ctx.enter_context(nc.psum_tensor("fb_ps", [P, EC, BLOCK], F32))
        pc = ctx.enter_context(nc.psum_tensor("fb_pc", [P, 2, BLOCK], F32))
        s_w, s_ws, s_xn, s_res = sem("s_w"), sem("s_ws"), sem("s_xn"), sem("s_res")
        s_h, s_t, s_f, s_split = sem("s_h"), sem("s_t"), sem("s_f"), sem("s_split")
        s_c, s_cs, s_out = sem("s_c"), sem("s_cs"), sem("s_out")
        block = ctx.enter_context(nc.Block())

        @block.scalar
        def _(act):
            norm_scalar(act, N1)
            norm_scalar(act, N2)

        @block.gpsimd
        def _(pool):
            pool.wait_ge(s_w, 32)
            flat = lambda w: w[:].rearrange("p a b c -> p (a b c)")
            pool_round(pool, flat(wh), raw[:], zero).then_inc(s_ws, 1)
            pool.wait_ge(s_ws, 1)
            pool.tensor_tensor(flat(wl), raw[:], flat(wh).bitcast(F32), ALU.subtract).then_inc(s_ws, 1)
            pool.wait_ge(s_xn, TILES)
            def one_block(k):
                pool.tensor_tensor(tile_of(x, k * BT, BT), tile_of(x, k * BT, BT),
                                   tile_of(xn, k * BT, BT), ALU.add).then_inc(s_res, 1)
            over_blocks(pool, one_block)
            pool.wait_ge(s_res, BLOCKS)

        @block.vector
        def _(dve):
            norm_vector(dve, N1, x)
            with dve.Fori(0, TILES) as i:
                normalise(dve, tile_of(xn, i), tile_of(x, i), N1, i).then_inc(s_xn, 1)
            dve.wait_ge(s_xn, TILES)
            norm_vector(dve, N2, xn)
            dve.wait_ge(s_w, 32)
            def one_block(k):
                wait(dve, s_t, k * EC)
                for j in range(BT):
                    normalise(dve, h[:, j, :], tile_of(xn, k * BT + j), N2, k * BT + j).then_inc(s_h, 1)
                wait(dve, s_c, k * 2)
                for c in range(EC):
                    wait(dve, s_t, k * EC + c + 1)
                    dve.tensor_scalar(hf[:, c, :], ps[:, c, :], affine[:, c:c + 1],
                                      affine[:, EC + c:EC + c + 1], ALU.mult, ALU.add).then_inc(s_f, 1)
                    wait(dve, s_f, k * EC + c + 1)
                    dve.tensor_copy(hT[:, 2 * c, :], hf[:, c, :]).then_inc(s_split, 1)
                    wait(dve, s_split, k * 2 * EC + 2 * c + 1)
                    dve.tensor_tensor(hT[:, 2 * c + 1, :], hf[:, c, :], hT[:, 2 * c, :].bitcast(F32),
                                      ALU.subtract).then_inc(s_split, 1)
                wait(dve, s_out, k * 16)
                for w in range(2):
                    wait(dve, s_c, k * 2 + w + 1)
                    dve.tensor_copy(cT[:, 2 * w, :], pc[:, w, :]).then_inc(s_cs, 1)
                    wait(dve, s_cs, k * 4 + 2 * w + 1)
                    dve.tensor_tensor(cT[:, 2 * w + 1, :], pc[:, w, :], cT[:, 2 * w, :].bitcast(F32),
                                      ALU.subtract).then_inc(s_cs, 1)
            over_blocks(dve, one_block)

        @block.tensor
        def _(pe):
            pe.wait_ge(s_ws, 2)
            def one_block(k):
                wait(pe, s_h, (k + 1) * BT)
                wait(pe, s_split, k * 2 * EC)
                for c in range(EC):
                    for j in range(BT):
                        mm = pe.transpose(ps[:, c, j * P:(j + 1) * P], h[:, j, c * P:(c + 1) * P], ident[:])
                    mm.then_inc(s_t, 1)
                wait(pe, s_split, (k + 1) * 2 * EC)
                wait(pe, s_cs, k * 4)
                for w in range(2):
                    prods = [(c, a, b) for c in range(EC) for a, b in ((wh, 0), (wh, 1), (wl, 0))]
                    for n, (c, a, b) in enumerate(prods):
                        mm = pe.matmul(pc[:, w, :], a[:, c, w, :], hT[:, 2 * c + b, :],
                                       start=n == 0, stop=n == len(prods) - 1)
                    mm.then_inc(s_c, 1)
            over_blocks(pe, one_block)

        @block.sync
        def _(sp):
            sp.dma_start(raw[:], w_down).then_inc(s_w, 16)
            sp.dma_start(affine[:], ln_affine).then_inc(s_w, 16)
            def one_block(k):
                wait(sp, s_cs, (k + 1) * 4)
                sp.dma_start(scratch[k // HALVES, :, :, bass.ds((k % HALVES) * BLOCK, BLOCK)].bitcast(F32),
                             cT[:].bitcast(F32)).then_inc(s_out, 16)
            over_blocks(sp, one_block)
            sp.wait_ge(s_out, 16 * BLOCKS)


def ffn(nc, name, x, ident, zero, w1, b1, w2, b2, out):
    with ExitStack() as ctx:
        sb = lambda n, shape, dt=F32: ctx.enter_context(nc.sbuf_tensor(f"{name}_{n}", shape, dt))
        sem = lambda n: ctx.enter_context(nc.semaphore(f"{name}_{n}"))
        N = norm_tensors(nc, ctx, f"{name}_n")
        GR = 3
        w1r, w1h, w1l = sb("w1r", [P, EC, FF]), sb("w1h", [P, EC, FF], F32R), sb("w1l", [P, EC, FF], F32R)
        w2r, w2h, w2l = sb("w2r", [P, FC, E]), sb("w2h", [P, FC, E], F32R), sb("w2l", [P, FC, E], F32R)
        b1s, b2s = sb("b1s", [P, FC]), sb("b2s", [P, E])
        h = sb("h", [P, BT, E])
        hT = sb("hT", [P, 2 * EC, BLOCK], F32R)
        g = sb("g", [P, GR, BLOCK])
        gh, gl = sb("gh", [P, GR, BLOCK], F32R), sb("gl", [P, GR, BLOCK], F32R)
        pt = ctx.enter_context(nc.psum_tensor(f"{name}_pt", [P, EC, BLOCK], F32))
        pf = ctx.enter_context(nc.psum_tensor(f"{name}_pf", [P, 2, BLOCK], F32))
        py = ctx.enter_context(nc.psum_tensor(f"{name}_py", [P, BT, BLOCK], F32))
        s_w, s_ws, s_h, s_t, s_split = (sem(n) for n in ("s_w", "s_ws", "s_h", "s_t", "s_split"))
        s_f, s_g, s_gs, s_yf, s_xa = (sem(n) for n in ("s_f", "s_g", "s_gs", "s_yf", "s_xa"))
        s_b, s_out = sem("s_b"), sem("s_out")
        block = ctx.enter_context(nc.Block())

        @block.sync
        def _(sp):
            sp.dma_start(w1r[:], w1.rearrange("(c p) f -> p c f", p=P)).then_inc(s_w, 16)
            sp.dma_start(w2r[:], w2.rearrange("(c p) f -> p c f", p=P)).then_inc(s_w, 16)
            sp.dma_start(b1s[:], b1).then_inc(s_w, 16)
            sp.dma_start(b2s[:], b2.partition_broadcast(P)).then_inc(s_w, 16)
            if out is not None:
                tiles = out.rearrange("(n p) e -> p n e", p=P)
                def one_block(k):
                    wait(sp, s_xa, (k + 1) * BT)
                    sp.dma_start(tiles[:, bass.ds(k * BT, BT), :], x[:, bass.ds(k * BT, BT), :]).then_inc(s_out, 16)
                over_blocks(sp, one_block)
                sp.wait_ge(s_out, 16 * BLOCKS)

        @block.gpsimd
        def _(pool):
            pool.wait_ge(s_w, 64)
            link = Chain(pool, s_ws)
            for r, hi, lo in ((w1r, w1h, w1l), (w2r, w2h, w2l)):
                link(pool_round(pool, hi[:].rearrange("p a b -> p (a b)"), r[:].rearrange("p a b -> p (a b)"), zero))
                link(pool.tensor_tensor(lo[:], r[:], hi[:].bitcast(F32), ALU.subtract))
            def one_block(k):
                wait(pool, s_h, (k + 1) * BT)
                xs = x[:, bass.ds(k * BT, BT), :]
                pool.tensor_tensor(xs, xs, b2s[:].unsqueeze(1).to_broadcast([P, BT, E]), ALU.add).then_inc(s_b, 1)
            over_blocks(pool, one_block)

        @block.scalar
        def _(act):
            norm_scalar(act, N)
            act.wait_ge(s_w, 64)
            def one_block(k):
                for f in range(FC):
                    wait(act, s_f, k * FC + f + 1)
                    if f >= GR:
                        wait(act, s_gs, k * 2 * FC + 2 * (f - GR) + 2)
                    else:
                        wait(act, s_gs, k * 2 * FC)
                    act.activation(g[:, f % GR, :], pf[:, f % 2, :], ACT.Gelu,
                                   bias=b1s[:, f:f + 1]).then_inc(s_g, 1)
            over_blocks(act, one_block)

        @block.vector
        def _(dve):
            norm_vector(dve, N, x)
            def one_block(k):
                wait(dve, s_t, k * EC)
                for j in range(BT):
                    normalise(dve, h[:, j, :], tile_of(x, k * BT + j), N, k * BT + j).then_inc(s_h, 1)
                wait(dve, s_f, k * FC)
                for c in range(EC):
                    wait(dve, s_t, k * EC + c + 1)
                    dve.tensor_copy(hT[:, 2 * c, :], pt[:, c, :]).then_inc(s_split, 1)
                    wait(dve, s_split, k * 2 * EC + 2 * c + 1)
                    dve.tensor_tensor(hT[:, 2 * c + 1, :], pt[:, c, :], hT[:, 2 * c, :].bitcast(F32),
                                      ALU.subtract).then_inc(s_split, 1)
                for f in range(FC):
                    wait(dve, s_g, k * FC + f + 1)
                    if f >= GR:
                        wait(dve, s_yf, k * FC + f - GR + 1)
                    dve.tensor_copy(gh[:, f % GR, :], g[:, f % GR, :]).then_inc(s_gs, 1)
                    wait(dve, s_gs, k * 2 * FC + 2 * f + 1)
                    dve.tensor_tensor(gl[:, f % GR, :], g[:, f % GR, :], gh[:, f % GR, :].bitcast(F32),
                                      ALU.subtract).then_inc(s_gs, 1)
                wait(dve, s_yf, (k + 1) * FC)
                wait(dve, s_b, k + 1)
                for j in range(BT):
                    dve.tensor_tensor(tile_of(x, k * BT + j), tile_of(x, k * BT + j), py[:, j, 0:E],
                                      ALU.add).then_inc(s_xa, 1)
            over_blocks(dve, one_block)

        @block.tensor
        def _(pe):
            pe.wait_ge(s_ws, 4)
            def one_block(k):
                wait(pe, s_h, (k + 1) * BT)
                wait(pe, s_split, k * 2 * EC)
                for c in range(EC):
                    for j in range(BT):
                        mm = pe.transpose(pt[:, c, j * P:(j + 1) * P], h[:, j, c * P:(c + 1) * P], ident[:])
                    mm.then_inc(s_t, 1)
                wait(pe, s_split, (k + 1) * 2 * EC)
                for f in range(FC + 2):
                    if f < FC:
                        if f >= 2:
                            wait(pe, s_g, k * FC + f - 1)
                        else:
                            wait(pe, s_g, k * FC)
                        cols = slice(f * P, (f + 1) * P)
                        prods = [(c, a, b) for c in range(EC) for a, b in ((w1h, 0), (w1h, 1), (w1l, 0))]
                        for n, (c, a, b) in enumerate(prods):
                            mm = pe.matmul(pf[:, f % 2, :], a[:, c, cols], hT[:, 2 * c + b, :],
                                           start=n == 0, stop=n == len(prods) - 1)
                        mm.then_inc(s_f, 1)
                    if f >= 2:
                        y = f - 2
                        wait(pe, s_gs, k * 2 * FC + 2 * y + 2)
                        if y == 0:
                            wait(pe, s_xa, k * BT)
                        for j in range(BT):
                            rows = slice(j * P, (j + 1) * P)
                            for n, (a, w) in enumerate(((gh, w2h), (gh, w2l), (gl, w2h))):
                                mm = pe.matmul(py[:, j, 0:E], a[:, y % GR, rows], w[:, y, :],
                                               start=y == 0 and n == 0, stop=y == FC - 1 and n == 2)
                        mm.then_inc(s_yf, 1)
            over_blocks(pe, one_block)


def attention(nc, name, x, ident, zero, scratch, w_qkv, w_out, scale, rope):
    with ExitStack() as ctx:
        sb = lambda n, shape, dt=F32: ctx.enter_context(nc.sbuf_tensor(f"{name}_{n}", shape, dt))
        psum = lambda n, shape: ctx.enter_context(nc.psum_tensor(f"{name}_{n}", shape, F32))
        sem = lambda n: ctx.enter_context(nc.semaphore(f"{name}_{n}"))
        WC = w_qkv.shape[2]
        NQ = 8 if rope is not None else 4
        if rope is not None:
            unit_steps = {1: 0, 2: 1, 3: 2, 5: 3, 6: 4, 7: 5, 9: 6, 10: 7}
            v_steps = {11: 0, 13: 1}
            convert_steps = {3: 0, 6: 1, 8: 2, 11: 3}
        else:
            unit_steps = {1: 0, 2: 1, 3: 2, 5: 3}
            v_steps = {6: 0, 7: 1}
            convert_steps = {1: 0, 2: 1, 3: 2, 5: 3}

        hT = sb("hT", [P, 4, S], F32R)
        wraw, woraw = sb("wraw", [P, WC]), sb("woraw", [P, E])
        wh, wl = sb("wh", [P, 2, WC], F32R), sb("wl", [P, 2, WC], F32R)
        woh, wol = sb("woh", [P, 2, E], F32R), sb("wol", [P, 2, E], F32R)
        nat_h, nat_l = sb("nat_h", [P, 2, BLOCK], F32R), sb("nat_l", [P, 2, BLOCK], F32R)
        q_h = sb("q_h", [P, 2, 2, S], F32R)
        q_l = sb("q_l", [P, 2, 2, S], F32R)
        k_s = sb("k_s", [P, 2, 2, S], F32R)
        v = sb("v", [P, 2, KT, P])
        p = sb("p", [P, PRING, S])
        pT = sb("pT", [P, 2, 2, KT, GW])
        nmax = sb("nmax", [P, NM])
        rsum, rinv = sb("rsum", [P, 2 * GS]), sb("rinv", [P, 2 * GS])
        r_sb = sb("r_sb", [P, GW])
        o_sb = sb("o_sb", [P, 2, GW])
        o_h, o_l = sb("o_h", [P, 2, GW], F32R), sb("o_l", [P, 2, GW], F32R)
        if rope is not None:
            cos_t, sin_t = sb("cos_t", [P, S]), sb("sin_t", [P, S])
            rot_a, rot_b, rot = sb("rot_a", [P, BLOCK]), sb("rot_b", [P, BLOCK]), sb("rot", [P, BLOCK])

        ps_s = psum("ps_s", [P, 2, S])
        ps_t = psum("ps_t", [P, 2, 4, P])
        ps_o = psum("ps_o", [P, 2 * GW])
        ps_m = psum("ps_m", [P, BLOCK])

        s_ht, s_raw, s_rawo = sem("s_ht"), sem("s_raw"), sem("s_rawo")
        s_rope = sem("s_rope")
        s_wsplit, s_wosplit = sem("s_wsplit"), sem("s_wosplit")
        s_proj, s_rot, s_rr, s_nat = sem("s_proj"), sem("s_rot"), sem("s_rr"), sem("s_nat")
        s_vp, s_v = sem("s_vp"), sem("s_v")
        s_stack = [sem("s_stack0"), sem("s_stack1")]
        s_scores, s_max, s_exp, s_tr, s_tev = (sem(n) for n in ("s_scores", "s_max", "s_exp", "s_tr", "s_tev"))
        s_recip, s_pv, s_rc, s_oev, s_osplit = (sem(n) for n in ("s_recip", "s_pv", "s_rc", "s_oev", "s_osplit"))
        s_wo, s_x = sem("s_wo"), sem("s_x")
        QD, KD = 8, 4
        SD = 16 * (QD + KD)

        def live(t, per_body, c, total):
            return not isinstance(t, int) or 0 <= per_body * t + c < total

        def wait_for(eng, s, t, per_body, c):
            wait(eng, s, t * per_body + c)

        def users(t, u):
            for s in range(STEPS):
                c = STEPS * u + s
                if s % GS == 0:
                    g = (c - WO_LAG) // GS
                    if live(t, 2 * PG, g, NGROUP):
                        yield s, (s_x, 2 * PG, g + 1)
                elif s in unit_steps and live(t, 2, u + 1, NPAIR):
                    j = unit_steps[s]
                    if rope is not None:
                        yield s, (s_rot, 2 * NQ, NQ * (u + 1) + j + 1)
                    else:
                        yield s, (s_nat, 2 * 8, 8 * (u + 1) + 2 * j + 2)
                elif s in v_steps and live(t, 2, u + 1, NPAIR):
                    yield s, (s_v, 2 * 2, 2 * (u + 1) + v_steps[s] + 1)

        def wait_ps_m(pe, t, u, s):
            last = None
            for at, (sm, per_body, c) in users(t, u):
                if at >= s:
                    break
                last = (sm, per_body, c)
            if last is None:
                tt, uu = (t, 0) if u == 1 else (t - 1, 1)
                for at, (sm, per_body, c) in users(tt, uu):
                    last = (sm, per_body, c if u == 1 else c - per_body)
            if last is not None:
                wait_for(pe, last[0], t, last[1], last[2])

        def scores(pe, t, c):
            par, buf, cc = (c // STEPS) % 2, c % 2, c % STEPS
            head, qt = (cc % GS) // GQ, GQ * (cc // GS) + cc % GQ
            if cc == 0:
                pair = c // STEPS
                for s in s_stack:
                    wait_for(pe, s, t, 2 * SD, SD * (pair + 1))
            wait_for(pe, s_exp, t, 2 * STEPS, c - 1)
            cols = slice(qt * P, (qt + 1) * P)
            for first, q in ((True, q_h), (False, q_l)):
                for kh in range(HALVES):
                    keys = slice(kh * BLOCK, (kh + 1) * BLOCK)
                    mm = pe.matmul(ps_s[:, buf, keys], q[:, par, head, cols], k_s[:, par, head, keys],
                                   start=first, stop=not first)
            mm.then_inc(s_scores, 1)

        def transposes(pe, t, c):
            wait_for(pe, s_exp, t, 2 * STEPS, c + 1)
            for h in range(2):
                wait_for(pe, s_tev, t, 4 * STEPS, 2 * c + h - 1)
                for k in range(4):
                    kt = 4 * h + k
                    mm = pe.transpose(ps_t[:, h, k, :], p[:, c % PRING, kt * P:(kt + 1) * P], ident[:])
                mm.then_inc(s_tr, 1)

        def pv(pe, t, g, j):
            par = (g // PG) % 2
            if j == 0:
                wait_for(pe, s_tev, t, 4 * STEPS, 2 * GS * (g + 1))
                wait_for(pe, s_oev, t, 2 * PG, g)
                wait_for(pe, s_v, t, 4, 2 * (g // PG + 1))
            for kt in range(2 * j, 2 * j + 2):
                for head in range(2):
                    rows = slice(D * head, D * (head + 1))
                    pe.matmul(ps_o[rows, 0:GW], v[:, par, kt, rows], pT[:, g % 2, head, kt, :],
                              start=kt == 0, stop=kt == KT - 1)
            if j == GS - 1:
                wait_for(pe, s_recip, t, 2 * PG, g + 1)
                for qi in range(GQ):
                    for head in range(2):
                        i = GS * (g % 2) + GQ * head + qi
                        mm = pe.matmul(ps_o[D * head:D * (head + 1), GW + qi * P:GW + (qi + 1) * P],
                                       rinv[:, i:i + 1].to_broadcast([P, D]), ident[:], start=True, stop=True)
                mm.then_inc(s_pv, 1)

        def out_project(pe, t, u, s, g):
            wait_for(pe, s_osplit, t, 4 * PG, 2 * g + 2)
            wait_for(pe, s_wosplit, t, 4, 2 * (g // PG + 1))
            wait_ps_m(pe, t, u, s)
            par = (g // PG) % 2
            for qi in range(GQ):
                rows = slice(qi * P, (qi + 1) * P)
                for n, (o, w) in enumerate(((o_h, woh), (o_h, wol), (o_l, woh))):
                    mm = pe.matmul(ps_m[:, qi * E:(qi + 1) * E], o[:, g % 2, rows], w[:, par, :],
                                   start=n == 0, stop=n == 2)
            mm.then_inc(s_wo, 1)

        def project_qk(pe, t, u, s, j):
            pair = u + 1
            if j == 0:
                wait_for(pe, s_ht, t, 16, 16 * (pair // 2 + 1))
                wait_for(pe, s_wsplit, t, 4, 2 * (pair + 1))
            wait_ps_m(pe, t, u, s)
            par = pair % 2
            if rope is not None:
                which, half, variant = j // 4, (j // 2) % 2, j % 2
                blocks = [(2 * which + variant, 2 * which)]
            else:
                which, half = j // 2, j % 2
                blocks = [(2 * which + c, 2 * c) for c in range(EC)]
            cols = slice(half * BLOCK, (half + 1) * BLOCK)
            prods = [(wb, fb, w, f) for wb, fb in blocks for w, f in ((wh, 0), (wh, 1), (wl, 0))]
            for n, (wb, fb, w, f) in enumerate(prods):
                mm = pe.matmul(ps_m[:, :], w[:, par, wb * P:(wb + 1) * P], hT[:, fb + f, cols],
                               start=n == 0, stop=n == len(prods) - 1)
            mm.then_inc(s_proj, 1)

        def project_v(pe, t, u, s, half):
            wait_ps_m(pe, t, u, s)
            par = (u + 1) % 2
            blocks = [(4, 2)] if rope is not None else [(4 + c, 2 * c) for c in range(EC)]
            prods = [(wb, fb, w, f) for wb, fb in blocks for w, f in ((wh, 0), (wh, 1), (wl, 0))]
            for i in range(4):
                kt = 4 * half + i
                for n, (wb, fb, w, f) in enumerate(prods):
                    mm = pe.matmul(ps_m[:, i * P:(i + 1) * P], hT[:, fb + f, kt * P:(kt + 1) * P],
                                   w[:, par, wb * P:(wb + 1) * P], start=n == 0, stop=n == len(prods) - 1)
            mm.then_inc(s_vp, 1)

        def pe_window(pe, t, u):
            for s in range(STEPS):
                c = STEPS * u + s
                if live(t, 2 * STEPS, c, NSTEP):
                    scores(pe, t, c)
                if live(t, 2 * STEPS, c - T_LAG, NSTEP):
                    transposes(pe, t, c - T_LAG)
                g = (c - WO_LAG) // GS
                if s % GS == 0 and live(t, 2 * PG, g, NGROUP):
                    out_project(pe, t, u, s, g)
                if s in unit_steps and live(t, 2, u + 1, NPAIR):
                    project_qk(pe, t, u, s, unit_steps[s])
                if s in v_steps and live(t, 2, u + 1, NPAIR):
                    project_v(pe, t, u, s, v_steps[s])
                g, j = (c - PV_LAG) // GS, (c - PV_LAG) % GS
                if live(t, 2 * PG, g, NGROUP):
                    pv(pe, t, g, j)

        def convert(dve, t, u, jj, src):
            pair, which, half = u + 1, jj // 2, jj % 2
            wait_for(dve, s_stack[half], t, 2 * SD, SD * pair + (16 * QD if which else 0))
            mul = scale if which == 0 else 1.0
            dve.tensor_scalar(nat_h[:, half, :], src, mul, None, ALU.mult).then_inc(s_nat, 1)
            wait_for(dve, s_nat, t, 16, 8 * pair + 2 * jj + 1)
            dve.scalar_tensor_tensor(nat_l[:, half, :], src, mul, nat_h[:, half, :].bitcast(F32),
                                     ALU.mult, ALU.subtract).then_inc(s_nat, 1)

        def dve_window(dve, t, u):
            for s in range(STEPS):
                c = STEPS * u + s
                g = (c - O_LAG) // GS
                if c % GS == O_LAG % GS and live(t, 2 * PG, g, NGROUP):
                    wait_for(dve, s_pv, t, 2 * PG, g + 1)
                    wait_for(dve, s_oev, t, 2 * PG, g)
                    dve.tensor_copy(r_sb[:], ps_o[:, GW:2 * GW]).then_inc(s_rc, 1)
                    wait_for(dve, s_rc, t, 2 * PG, g + 1)
                    wait_for(dve, s_osplit, t, 4 * PG, 2 * (g - 1))
                    dve.tensor_tensor(o_sb[:, g % 2, :], ps_o[:, 0:GW], r_sb[:], ALU.mult).then_inc(s_oev, 1)
                if live(t, 2 * STEPS, c, NSTEP):
                    wait_for(dve, s_scores, t, 2 * STEPS, c + 1)
                    dve.reduce_max(nmax[:, c % NM:c % NM + 1], ps_s[:, c % 2, :], AX_X,
                                   negate=True).then_inc(s_max, 1)
                g = (c - PV_LAG) // GS
                if c % GS == PV_LAG % GS and live(t, 2 * PG, g, NGROUP):
                    wait_for(dve, s_exp, t, 2 * STEPS, GS * (g + 1))
                    sl = slice(GS * (g % 2), GS * (g % 2) + GS)
                    dve.reciprocal(rinv[:, sl], rsum[:, sl]).then_inc(s_recip, 1)
                if s in convert_steps and rope is not None and live(t, 2, u + 1, NPAIR):
                    jj = convert_steps[s]
                    wait_for(dve, s_rr, t, 8, 4 * (u + 1) + jj + 1)
                    convert(dve, t, u, jj, rot[:])
                if s in unit_steps and live(t, 2, u + 1, NPAIR):
                    j = unit_steps[s]
                    wait_for(dve, s_proj, t, 2 * NQ, NQ * (u + 1) + j + 1)
                    if rope is None:
                        convert(dve, t, u, j, ps_m[:, :])
                    else:
                        half, variant = (j // 2) % 2, j % 2
                        wait_for(dve, s_rr, t, 8, 4 * (u + 1) + j // 2)
                        cols = slice(half * BLOCK, (half + 1) * BLOCK)
                        dve.tensor_tensor((rot_b if variant else rot_a)[:], ps_m[:, :],
                                          (sin_t if variant else cos_t)[:, cols], ALU.mult).then_inc(s_rot, 1)
                if s in v_steps and live(t, 2, u + 1, NPAIR):
                    half = v_steps[s]
                    wait_for(dve, s_vp, t, 4, 2 * (u + 1) + half + 1)
                    wait_for(dve, s_pv, t, 2 * PG, PG * u)
                    dve.tensor_copy(v[:, (u + 1) % 2, 4 * half:4 * half + 4, :],
                                    ps_m[:, :].rearrange("p (a b) -> p a b", b=P)).then_inc(s_v, 1)
                g = (c - WO_LAG) // GS
                if s % GS == 0 and live(t, 2 * PG, g, NGROUP):
                    wait_for(dve, s_wo, t, 2 * PG, g + 1)
                    body = t if g >= 0 else t - 1
                    tile = (body // (PAIRS // 2)) * KT + GQ * (g % PG)
                    xs = tile_of(x, tile, GQ)
                    dve.tensor_tensor(xs, xs, ps_m[:, :], ALU.add).then_inc(s_x, 1)

        def act_window(act, t, u):
            for s in range(STEPS):
                c = STEPS * u + s
                b = c - T_LAG
                if live(t, 2 * STEPS, b, NSTEP):
                    g, head, qi = b // GS, (b % GS) // GQ, b % GQ
                    for h in range(2):
                        wait_for(act, s_tr, t, 4 * STEPS, 2 * b + h + 1)
                        if b % GS == 0 and h == 0:
                            wait_for(act, s_pv, t, 2 * PG, g - 1)
                        act.activation(pT[:, g % 2, head, 4 * h:4 * h + 4, qi * P:(qi + 1) * P],
                                       ps_t[:, h, :, :], ACT.Copy).then_inc(s_tev, 1)
                if live(t, 2 * STEPS, c, NSTEP):
                    wait_for(act, s_max, t, 2 * STEPS, c + 1)
                    wait_for(act, s_tr, t, 4 * STEPS, 2 * (c - PRING) + 2)
                    act.activation(p[:, c % PRING, :], ps_s[:, c % 2, :], ACT.Exp,
                                   bias=nmax[:, c % NM:c % NM + 1],
                                   accum_out=rsum[:, c % (2 * GS):c % (2 * GS) + 1]).then_inc(s_exp, 1)

        def split_qkv(pool, t, par, pair):
            wait_for(pool, s_raw, t, 32, 16 * (pair + 1))
            wait_for(pool, s_vp, t, 4, 2 * (pair - 1))
            pool_round(pool, wh[:, par, :], wraw[:], zero).then_inc(s_wsplit, 1)
            wait_for(pool, s_wsplit, t, 4, 2 * pair + 1)
            pool.tensor_tensor(wl[:, par, :], wraw[:], wh[:, par, :].bitcast(F32),
                               ALU.subtract).then_inc(s_wsplit, 1)

        def pool_window(pool, t, u):
            for s in range(STEPS):
                c = STEPS * u + s
                g = (c - O_LAG) // GS
                if c % GS == O_LAG % GS and live(t, 2 * PG, g, NGROUP):
                    wait_for(pool, s_oev, t, 2 * PG, g + 1)
                    wait_for(pool, s_wo, t, 2 * PG, g - 1)
                    pool_round(pool, o_h[:, g % 2, :], o_sb[:, g % 2, :], zero).then_inc(s_osplit, 1)
                    wait_for(pool, s_osplit, t, 4 * PG, 2 * g + 1)
                    pool.tensor_tensor(o_l[:, g % 2, :], o_sb[:, g % 2, :], o_h[:, g % 2, :].bitcast(F32),
                                       ALU.subtract).then_inc(s_osplit, 1)
                if rope is not None and s in unit_steps and unit_steps[s] % 2 and live(t, 2, u + 1, NPAIR):
                    jj = unit_steps[s] // 2
                    wait_for(pool, s_rot, t, 2 * NQ, NQ * (u + 1) + 2 * jj + 2)
                    wait_for(pool, s_nat, t, 16, 8 * (u + 1) + 2 * jj)
                    pool.tensor_tensor(rot[:], rot_a[:], rot_b[:], ALU.add).then_inc(s_rr, 1)
                if s == 3 and live(t, 2, u + 2, NPAIR):
                    split_qkv(pool, t, u, u + 2)
                if s == 11 and live(t, 2, u + 1, NPAIR):
                    pair = u + 1
                    wait_for(pool, s_rawo, t, 32, 16 * (pair + 1))
                    wait_for(pool, s_wo, t, 2 * PG, PG * (pair - 1))
                    pool_round(pool, woh[:, pair % 2, :], woraw[:], zero).then_inc(s_wosplit, 1)
                    wait_for(pool, s_wosplit, t, 4, 2 * pair + 1)
                    pool.tensor_tensor(wol[:, pair % 2, :], woraw[:], woh[:, pair % 2, :].bitcast(F32),
                                       ALU.subtract).then_inc(s_wosplit, 1)

        def pair_of_batch(t, pair):
            return ((t + pair // 2) % (PAIRS // 2)) * 2 + pair % 2

        def sp_window(sp, t, u):
            if live(t, 2, u + 2, NPAIR):
                source = pair_of_batch(t, u + 2)
                wait_for(sp, s_wsplit, t, 4, 2 * (u + 2))
                sp.dma_start(wraw[:], w_qkv[source]).then_inc(s_raw, 16)
            if live(t, 2, u + 1, NPAIR):
                pair = u + 1
                par = pair % 2
                source = pair_of_batch(t, pair)
                wait_for(sp, s_wosplit, t, 4, 2 * pair)
                sp.dma_start(woraw[:], w_out[source]).then_inc(s_rawo, 16)
                for jj in range(4):
                    which, half = jj // 2, jj % 2
                    cols = slice(half * BLOCK, (half + 1) * BLOCK)
                    wait_for(sp, s_nat, t, 16, 8 * pair + 2 * jj + 2)
                    parts = [(q_h, nat_h, nat_h), (q_l, nat_l, nat_l)] if which == 0 else [(k_s, nat_h, nat_l)]
                    for dst, top, bottom in parts:
                        for head in range(2):
                            rows = slice(D * head, D * (head + 1))
                            for r, src in ((0, top), (D, bottom)):
                                sp.dma_start(dst[r:r + D, par, head, cols].bitcast(F32),
                                             src[rows, half, :].bitcast(F32)).then_inc(s_stack[half], 16)
            if u == 0 and live(t, 1, 1, BODIES):
                source = (t + 1) // (PAIRS // 2)
                wait_for(sp, s_vp, t, 4, 2 * 2)
                sp.dma_start(hT[:].bitcast(F32), scratch[source].bitcast(F32)).then_inc(s_ht, 16)

        def run(eng, window):
            window(eng, -1, 1)
            for u in range(2):
                window(eng, 0, u)
            with eng.Fori(1, BODIES - 1) as t:
                for u in range(2):
                    window(eng, t, u)
            for u in range(2):
                window(eng, BODIES - 1, u)
            window(eng, BODIES, 0)

        block = ctx.enter_context(nc.Block())

        @block.sync
        def _(sp):
            sp.dma_start(hT[:].bitcast(F32), scratch[0].bitcast(F32)).then_inc(s_ht, 16)
            sp.dma_start(wraw[:], w_qkv[0]).then_inc(s_raw, 16)
            if rope is not None:
                sp.dma_start(cos_t[:], rope[0]).then_inc(s_rope, 16)
                sp.dma_start(sin_t[:], rope[1]).then_inc(s_rope, 16)
            run(sp, sp_window)

        @block.gpsimd
        def _(pool):
            split_qkv(pool, 0, 0, 0)
            run(pool, pool_window)

        @block.vector
        def _(dve):
            if rope is not None:
                dve.wait_ge(s_rope, 32)
            run(dve, dve_window)

        @block.scalar
        def _(act):
            run(act, act_window)

        @block.tensor
        def _(pe):
            run(pe, pe_window)


def hybrid_stack(nc, x_in, wa_qkv, wa_out, wb_down, ln_affine, wb_qkv, wb_out, rope, w1, b1, w2, b2, out):
    feat_a = nc.dram_tensor("feat_a", [B, P, 4, S], F32R).ap()
    feat_b = nc.dram_tensor("feat_b", [B, P, 4, S], F32R).ap()
    with ExitStack() as ctx:
        x = ctx.enter_context(nc.sbuf_tensor("x", [P, TILES, E], F32))
        ident = ctx.enter_context(nc.sbuf_tensor("ident", [P, P], F32))
        zero = ctx.enter_context(nc.sbuf_tensor("zero", [P, 1], F32))
        s_load, s_id = ctx.enter_context(nc.semaphore("s_load")), ctx.enter_context(nc.semaphore("s_id"))
        with nc.Block() as block:
            @block.sync
            def _(sp):
                tiles = x_in.rearrange("(n p) e -> p n e", p=P)
                for q in range(4):
                    part = slice(q * TILES // 4, (q + 1) * TILES // 4)
                    sp.dma_start(x[:, part, :], tiles[:, part, :]).then_inc(s_load, 16)
                sp.wait_ge(s_load, 64)

            @block.gpsimd
            def _(pool):
                pool.memset(ident[:], 0.0).then_inc(s_id, 1)
                pool.wait_ge(s_id, 1)
                pool.affine_select(out=ident[:], in_=ident[:], compare_op=ALU.not_equal, fill=1.0, base=0,
                                   pattern=[[-1, P]], channel_multiplier=1).then_inc(s_id, 1)
                pool.memset(zero[:], 0.0).then_inc(s_id, 1)
                pool.wait_ge(s_id, 3)

        features_a(nc, x, ident, feat_a)
        attention(nc, "a", x, ident, zero, feat_a, wa_qkv, wa_out, 1.0 / (D * D * H), None)
        ffn(nc, "f1", x, ident, zero, w1, b1, w2, b2, None)
        features_b(nc, x, ident, zero, feat_b, wb_down, ln_affine)
        attention(nc, "b", x, ident, zero, feat_b, wb_qkv, wb_out, 1.0 / D ** 0.5, rope)
        ffn(nc, "f2", x, ident, zero, w1, b1, w2, b2, out)


def rope_tables():
    inv_freq = 1.0 / 10000.0 ** (np.arange(0, D, 2, dtype=np.float32) / D)
    freqs = np.outer(np.arange(S, dtype=np.float32), inv_freq)
    cos = np.concatenate([np.cos(freqs), np.cos(freqs)], -1)[:, ::2]
    sin = np.concatenate([np.sin(freqs), np.sin(freqs)], -1)[:, ::2]
    rows = np.arange(P)
    sign = np.where(rows % 2 == 0, -1.0, 1.0).astype(np.float32)
    pick = (rows % D) // 2
    return np.ascontiguousarray(np.stack([cos.T[pick], sin.T[pick] * sign[:, None]]).astype(np.float32))


def kernel(**inputs):
    import concourse.bacc as bacc
    from concourse.bass_utils import run_bass_kernel_spmd

    g = {k: np.asarray(v) for k, v in inputs.items()}
    ka = g["L0_attn_a_kernel"].reshape(3, PAIRS, 2, EC, P, D)
    wa_qkv = ka.transpose(1, 4, 0, 3, 2, 5).reshape(PAIRS, P, 3 * EC * P)
    wa_out = g["L0_attn_a_WO"][0].reshape(D, PAIRS, 2, E).transpose(1, 2, 0, 3).reshape(PAIRS, P, E)
    up = {n: g["L0_attn_b_w_up_" + n].reshape(PAIRS, P, P) for n in "qkv"}
    partner = np.arange(P) ^ 1
    blocks = [up["q"], up["q"][:, partner], up["k"], up["k"][:, partner], up["v"]]
    wb_qkv = np.stack(blocks, 1).transpose(0, 3, 1, 2).reshape(PAIRS, P, 5 * P)
    wb_out = g["L0_attn_b_w_out"].T.reshape(PAIRS, P, E)
    down = np.stack([g["L0_attn_b_w_down_q"], g["L0_attn_b_w_down_kv"]])
    wb_down = down.reshape(2, P, EC, P).transpose(3, 2, 0, 1).reshape(P, EC * 2 * P)
    ln_affine = np.stack([g["L0_attn_b_ln_scale"], g["L0_attn_b_ln_bias"]]).reshape(2 * EC, P).T
    arrays = {
        "x_in": g["L0_attn_a_x"].reshape(B * S, E), "wa_qkv": wa_qkv, "wa_out": wa_out,
        "wb_down": wb_down, "ln_affine": ln_affine, "wb_qkv": wb_qkv, "wb_out": wb_out,
        "rope": rope_tables(), "w1": g["L0_ffn_w1"], "b1": g["L0_ffn_b1"].reshape(FC, P).T,
        "w2": g["L0_ffn_w2"], "b2": g["L0_ffn_b2"],
    }
    arrays = {k: np.ascontiguousarray(a) for k, a in arrays.items()}
    nc = bacc.Bacc("TRN2", target_bir_lowering=False, num_devices=1)
    aps = {k: nc.dram_tensor(k, a.shape, mybir.dt.from_np(a.dtype), kind="ExternalInput").ap()
           for k, a in arrays.items()}
    out = nc.dram_tensor("out", (B * S, E), F32, kind="ExternalOutput").ap()
    hybrid_stack(nc, out=out, **aps)
    r = run_bass_kernel_spmd(nc, [arrays], core_ids=[0])
    return r.results[0]["out"].reshape(B, S, E)
```

```python
from contextlib import ExitStack

import numpy as np

import concourse.bass as bass
from concourse import mybir

F32 = mybir.dt.float32
F32R = mybir.dt.float32r
ACT = mybir.ActivationFunctionType
ALU = mybir.AluOpType
AX_X = mybir.AxisListType.X

P = 128
B, S, E = 4, 1024, 256
H, D = 16, 64
FF = 1024
TILES = B * S // P
BLOCK = 512
BLOCKS = B * S // BLOCK
BT = BLOCK // P
EC = E // P
FC = FF // P
KT = S // P
HALVES = S // BLOCK
EPS = 1e-5

PAIRS = H // 2
NPAIR = B * PAIRS
STEPS = 2 * KT
NSTEP = NPAIR * STEPS
GQ = 2
GW = GQ * P
GS = 2 * GQ
PG = STEPS // GS
NGROUP = NPAIR * PG
BODIES = NPAIR // 2
PRING = 4
NM = 4
N_LAG, T_LAG, PV_LAG, O_LAG, WO_LAG = 2, 3, 7, 11, 12
assert B % 2 == 0 and PAIRS % 2 == 0 and PG == 4 and GS == 4


class Chain:

    def __init__(self, eng, sem):
        self.eng, self.sem, self.n = eng, sem, 0

    def __call__(self, ins):
        self.n += 1
        ins.then_inc(self.sem, 1)
        self.eng.wait_ge(self.sem, self.n)


def wait(eng, sem, value):
    if not isinstance(value, int) or value > 0:
        eng.wait_ge(sem, value)


def live(t, per_body, c, total):
    return not isinstance(t, int) or 0 <= per_body * t + c < total


def wait_for(eng, sem, t, per_body, c):
    wait(eng, sem, t * per_body + c)


def tile_of(tensor, index, count=1):
    return tensor[:, bass.ds(index, count), :].rearrange("p a b -> p (a b)")


def pool_round(pool, hi, src, zero):
    return pool.tensor_tensor(hi, src, zero[:].to_broadcast(list(src.shape)), ALU.add)


def split3(w_hi, w_lo):
    return (w_hi, 0), (w_lo, 0), (w_hi, 1)


class BlockNorm:

    def __init__(self, nc, ctx, name, consts):
        sb = lambda n, shape: ctx.enter_context(nc.sbuf_tensor(f"{name}_{n}", shape, F32))
        sem = lambda n: ctx.enter_context(nc.semaphore(f"{name}_{n}"))
        self.consts = consts
        self.parts = sb("parts", [P, BT, 2, 3])
        self.both, self.diff, self.sq = sb("both", [P, BT, 3]), sb("diff", [P, BT]), sb("sq", [P, BT])
        self.var = sb("var", [P, BT])
        self.ve, self.rstd, self.shift = sb("ve", [P, BT]), sb("rstd", [P, BT]), sb("shift", [P, BT])
        self.s_stats, self.s_rstd, self.s_shift = sem("s_stats"), sem("s_rstd"), sem("s_shift")
        self.s_var = sem("s_var")

    def stats(self, dve, t, c, src):
        for j in range(BT):
            dve.bn_stats(self.parts[:, j, :, :].rearrange("p a b -> p (a b)"), src(j)).then_inc(self.s_stats, 1)
        even, odd = self.parts[:, :, 0, :], self.parts[:, :, 1, :]
        wait_for(dve, self.s_stats, t, 2 * BT, BT * (c + 1))
        dve.tensor_tensor(self.diff[:], even[:, :, 1], odd[:, :, 1], ALU.subtract).then_inc(self.s_var, 1)
        dve.tensor_tensor(self.both[:], even, odd, ALU.add).then_inc(self.s_var, 1)
        wait_for(dve, self.s_var, t, 8, 4 * c + 1)
        dve.scalar_tensor_tensor(self.sq[:], self.diff[:], 0.25, self.diff[:],
                                 ALU.mult, ALU.mult).then_inc(self.s_var, 1)
        wait_for(dve, self.s_var, t, 8, 4 * c + 3)
        dve.scalar_tensor_tensor(self.var[:], self.both[:, :, 2], 1.0 / E, self.sq[:],
                                 ALU.mult, ALU.add).then_inc(self.s_var, 1)

    def power(self, pool, t, c):
        zero, eps, minus_half = self.consts
        wait_for(pool, self.s_var, t, 8, 4 * (c + 1))
        pool.tensor_tensor(self.ve[:], self.var[:], eps[:].to_broadcast([P, BT]), ALU.add).then_inc(self.s_rstd, 1)
        wait_for(pool, self.s_rstd, t, 4, 2 * c + 1)
        pool.tensor_tensor(self.rstd[:], self.ve[:], minus_half[:].to_broadcast([P, BT]), ALU.pow).then_inc(self.s_rstd, 1)

    def shifts(self, dve, t, c):
        wait_for(dve, self.s_rstd, t, 4, 2 * c + 2)
        dve.scalar_tensor_tensor(self.shift[:], self.both[:, :, 1], -0.5, self.rstd[:],
                                 ALU.mult, ALU.mult).then_inc(self.s_shift, 1)
        wait_for(dve, self.s_shift, t, 2, c + 1)

    def apply(self, dve, j, dst, src):
        return dve.tensor_scalar(dst, src, self.rstd[:, j:j + 1], self.shift[:, j:j + 1], ALU.mult, ALU.add)


def run_bodies(eng, window, bodies, ahead):
    if ahead:
        window(eng, -1, 1)
    for u in range(2):
        window(eng, 0, u)
    with eng.Fori(1, bodies - 1) as t:
        for u in range(2):
            window(eng, t, u)
    for u in range(2):
        window(eng, bodies - 1, u)
    window(eng, bodies, 0)


def transpose_block(pe, dst, h, ident, done):
    for c in range(EC):
        for j in range(BT):
            mm = pe.transpose(dst[:, c, j * P:(j + 1) * P], h[:, j, c * P:(c + 1) * P], ident[:])
        mm.then_inc(done, 1)


def store_block(sp, scratch, t, c, src, done):
    u = c % 2
    sp.dma_start(scratch[t + c // 2, :, :, u * BLOCK:(u + 1) * BLOCK].bitcast(F32),
                 src.bitcast(F32)).then_inc(done, 16)


def features_a(nc, x_in, x, ident, consts, scratch):
    with ExitStack() as ctx:
        sb = lambda n, shape, dt=F32: ctx.enter_context(nc.sbuf_tensor(f"fa_{n}", shape, dt))
        sem = lambda n: ctx.enter_context(nc.semaphore(f"fa_{n}"))
        norm = BlockNorm(nc, ctx, "fa_n", consts)
        h = sb("h", [P, 2, BT, E])
        hT = sb("hT", [P, 2, 2 * EC, BLOCK], F32R)
        ps = ctx.enter_context(nc.psum_tensor("fa_ps", [P, 2, EC, BLOCK], F32))
        s_x, s_out = [sem("s_x0"), sem("s_x1")], [sem("s_out0"), sem("s_out1")]
        s_h, s_t, s_hi, s_lo = sem("s_h"), sem("s_t"), sem("s_hi"), sem("s_lo")
        tiles = x_in.rearrange("(n p) e -> p n e", p=P)

        def dve_window(dve, t, u):
            if live(t, 2, u, BLOCKS):
                wait_for(dve, s_x[u], t, 16, 16)
                dve.tensor_copy(h[:, u, :, :], x[:, bass.ds(t * 2 * BT + u * BT, BT), :]).then_inc(s_h, 1)
                wait_for(dve, s_h, t, 2 * (BT + 1), (BT + 1) * u + 1)
                norm.stats(dve, t, u, lambda j: h[:, u, j, :])
            if live(t, 2, u - 1, BLOCKS):
                lo(dve, t, u - 1)
            if live(t, 2, u, BLOCKS):
                norm.shifts(dve, t, u)
                for j in range(BT):
                    norm.apply(dve, j, h[:, u, j, :], h[:, u, j, :]).then_inc(s_h, 1)

        def lo(dve, t, c):
            for k in range(EC):
                wait_for(dve, s_hi, t, 2 * EC, EC * c + k + 1)
                dve.tensor_tensor(hT[:, c % 2, 2 * k + 1, :], ps[:, c % 2, k, :],
                                  hT[:, c % 2, 2 * k, :].bitcast(F32), ALU.subtract).then_inc(s_lo, 1)

        def pool_window(pool, t, u):
            if live(t, 2, u, BLOCKS):
                norm.power(pool, t, u)

        def pe_window(pe, t, u):
            if live(t, 2, u, BLOCKS):
                wait_for(pe, s_h, t, 2 * (BT + 1), (BT + 1) * (u + 1))
                wait_for(pe, s_lo, t, 2 * EC, EC * (u - 1))
                transpose_block(pe, ps[:, u, :, :], h[:, u, :, :], ident, s_t)

        def act_window(act, t, u):
            if live(t, 2, u, BLOCKS):
                wait_for(act, s_out[u], t, 16, 0)
                for k in range(EC):
                    wait_for(act, s_t, t, 2 * EC, EC * u + k + 1)
                    act.activation(hT[:, u, 2 * k, :], ps[:, u, k, :], ACT.Copy).then_inc(s_hi, 1)

        def sp_window(sp, t, u):
            if live(t, 2, u, BLOCKS):
                wait_for(sp, s_x[u], t, 16, 0)
                sp.dma_start(x[:, bass.ds(t * 2 * BT + u * BT, BT), :],
                             tiles[:, bass.ds(t * 2 * BT + u * BT, BT), :]).then_inc(s_x[u], 16)
            if live(t, 2, u - 1, BLOCKS):
                wait_for(sp, s_lo, t, 2 * EC, EC * u)
                store_block(sp, scratch, t, u - 1, hT[:, (u - 1) % 2, :, :], s_out[(u - 1) % 2])

        block = ctx.enter_context(nc.Block())

        @block.sync
        def _(sp):
            run_bodies(sp, sp_window, BLOCKS // 2, False)
            for s in s_out:
                sp.wait_ge(s, 16 * BLOCKS // 2)

        @block.gpsimd
        def _(pool):
            run_bodies(pool, pool_window, BLOCKS // 2, False)

        @block.vector
        def _(dve):
            run_bodies(dve, dve_window, BLOCKS // 2, False)

        @block.scalar
        def _(act):
            run_bodies(act, act_window, BLOCKS // 2, False)

        @block.tensor
        def _(pe):
            run_bodies(pe, pe_window, BLOCKS // 2, False)


def ffn(nc, name, x, ident, consts, w1, b1, w2, b2, out=None, inner=None):
    with ExitStack() as ctx:
        sb = lambda n, shape, dt=F32: ctx.enter_context(nc.sbuf_tensor(f"{name}_{n}", shape, dt))
        psum = lambda n, shape: ctx.enter_context(nc.psum_tensor(f"{name}_{n}", shape, F32))
        sem = lambda n: ctx.enter_context(nc.semaphore(f"{name}_{n}"))
        LAG, GR = 3, 4
        CHUNKS = BLOCKS * FC
        norm = BlockNorm(nc, ctx, f"{name}_n", consts)
        w1r, w1h, w1l = sb("w1r", [P, EC, FF]), sb("w1h", [P, EC, FF], F32R), sb("w1l", [P, EC, FF], F32R)
        w2r, w2h, w2l = sb("w2r", [P, FC, E]), sb("w2h", [P, FC, E], F32R), sb("w2l", [P, FC, E], F32R)
        b1s, b2s = sb("b1s", [P, FC]), sb("b2s", [P, E])
        h = sb("h", [P, BT, E])
        hT = sb("hT", [P, 2, 2 * EC, BLOCK], F32R)
        g = sb("g", [P, GR, BLOCK])
        gh, gl = sb("gh", [P, GR, BLOCK], F32R), sb("gl", [P, GR, BLOCK], F32R)
        pt = psum("pt", [P, EC, BLOCK])
        pf = psum("pf", [P, 2, BLOCK])
        py = psum("py", [P, BT, BLOCK])
        s_w, s_b = sem("s_w"), sem("s_b")
        s_whi, s_wlo = sem("s_whi"), sem("s_wlo")
        s_h, s_t, s_hi, s_lo = sem("s_h"), sem("s_t"), sem("s_hi"), sem("s_lo")
        s_f, s_g, s_gh, s_gl, s_y, s_xa = (sem(n) for n in ("s_f", "s_g", "s_gh", "s_gl", "s_y", "s_xa"))
        s_out = sem("s_out")
        xnew = sb("xnew", [P, BT, E])
        if inner is not None:
            w_down, ln_affine, scratch = inner
            norm_x, norm_h = BlockNorm(nc, ctx, f"{name}_nx", consts), BlockNorm(nc, ctx, f"{name}_nh", consts)
            xn, h2 = sb("xn", [P, BT, E]), sb("h2", [P, BT, E])
            hf = sb("hf", [P, EC, BLOCK])
            h2T, cT = sb("h2T", [P, 2 * EC, BLOCK], F32R), sb("cT", [P, 4, BLOCK], F32R)
            wdr = sb("wdr", [P, EC * 2 * P])
            wdh, wdl = sb("wdh", [P, EC, 2, P], F32R), sb("wdl", [P, EC, 2, P], F32R)
            affine = sb("affine", [P, 2 * EC])
            s_wd, s_wds = sem("s_wd"), sem("s_wds")
            s_xn, s_h2, s_t2, s_hf, s_h2hi, s_h2lo = (sem(n) for n in ("s_xn", "s_h2", "s_t2", "s_hf", "s_h2hi", "s_h2lo"))
            s_c, s_chi, s_clo = sem("s_c"), sem("s_chi"), sem("s_clo")
        s_res = sem("s_res")

        def x_tile(t, c, j):
            return tile_of(x, t * 2 * BT + c * BT + j)

        def w1_products(pe, t, c):
            f, b = c % FC, c // FC
            if f == 0:
                wait_for(pe, s_lo, t, 2 * EC, EC * (b + 1))
            wait_for(pe, s_g, t, 2 * FC, c - 1)
            cols = slice(f * P, (f + 1) * P)
            prods = [(k, w, part) for k in range(EC) for w, part in split3(w1h, w1l)]
            for i, (k, w, part) in enumerate(prods):
                mm = pe.matmul(pf[:, c % 2, :], w[:, k, cols], hT[:, b % 2, 2 * k + part, :],
                               start=i == 0, stop=i == len(prods) - 1)
            mm.then_inc(s_f, 1)

        def w2_products(pe, t, c):
            f, b = c % FC, c // FC
            wait_for(pe, s_gl, t, 2 * FC, c + 1)
            for j in range(BT):
                if f == 0:
                    wait_for(pe, s_xa, t, 2 * BT, BT * (b - 1) + j + 1)
                rows = slice(j * P, (j + 1) * P)
                for i, (a, w) in enumerate(((gh, w2h), (gh, w2l), (gl, w2h))):
                    mm = pe.matmul(py[:, j, 0:E], a[:, c % GR, rows], w[:, f, :],
                                   start=f == 0 and i == 0, stop=f == FC - 1 and i == 2)
            mm.then_inc(s_y, 1)

        def pe_window(pe, t, u):
            for s in range(FC):
                c = FC * u + s
                if live(t, 2 * FC, c, CHUNKS):
                    w1_products(pe, t, c)
                if live(t, 2 * FC, c - LAG, CHUNKS):
                    w2_products(pe, t, c - LAG)
                if s == 0 and inner is not None and live(t, 2, u - 2, BLOCKS):
                    wait_for(pe, s_h2lo, t, 2 * EC, EC * (u - 1))
                    wait_for(pe, s_hf, t, 2 * EC, EC * (u - 1))
                    for which in range(2):
                        prods = [(k, w, part) for k in range(EC) for w, part in split3(wdh, wdl)]
                        for i, (k, w, part) in enumerate(prods):
                            mm = pe.matmul(pt[:, which, :], w[:, k, which, :], h2T[:, 2 * k + part, :],
                                           start=i == 0, stop=i == len(prods) - 1)
                        mm.then_inc(s_c, 1)
                if s == 2 and live(t, 2, u + 1, BLOCKS):
                    wait_for(pe, s_h, t, 2 * BT, BT * (u + 2))
                    if inner is not None:
                        wait_for(pe, s_clo, t, 4, 2 * (u - 1))
                    wait_for(pe, s_lo, t, 2 * EC, EC * (u + 1))
                    transpose_block(pe, pt, h, ident, s_t)
                if s == 6 and inner is not None and live(t, 2, u - 1, BLOCKS):
                    wait_for(pe, s_h2, t, 2 * BT, BT * u)
                    if live(t, 2, u + 1, BLOCKS):
                        wait_for(pe, s_lo, t, 2 * EC, EC * (u + 2))
                    else:
                        wait_for(pe, s_clo, t, 4, 2 * (u - 1))
                    transpose_block(pe, pt, h2, ident, s_t2)

        def act_window(act, t, u):
            for s in range(FC):
                c = FC * u + s
                if live(t, 2 * FC, c, CHUNKS):
                    f = c % FC
                    wait_for(act, s_f, t, 2 * FC, c + 1)
                    wait_for(act, s_gl, t, 2 * FC, c - GR + 1)
                    act.activation(g[:, c % GR, :], pf[:, c % 2, :], ACT.Gelu,
                                   bias=b1s[:, f:f + 1]).then_inc(s_g, 1)
                    wait_for(act, s_g, t, 2 * FC, c + 1)
                    wait_for(act, s_y, t, 2 * FC, c - GR + 1)
                    act.activation(gh[:, c % GR, :], g[:, c % GR, :], ACT.Copy).then_inc(s_gh, 1)
                if s == 1 and inner is not None and live(t, 2, u - 2, BLOCKS):
                    wait_for(act, s_out, t, 32, 16 * (u - 2))
                    for which in range(2):
                        wait_for(act, s_c, t, 4, 2 * (u - 2) + which + 1)
                        act.activation(cT[:, 2 * which, :], pt[:, which, :], ACT.Copy).then_inc(s_chi, 1)
                if s == 2 and live(t, 2, u + 1, BLOCKS):
                    wait_for(act, s_f, t, 2 * FC, FC * u)
                    for k in range(EC):
                        wait_for(act, s_t, t, 2 * EC, EC * (u + 1) + k + 1)
                        act.activation(hT[:, (u + 1) % 2, 2 * k, :], pt[:, k, :], ACT.Copy).then_inc(s_hi, 1)
                if s == 6 and inner is not None and live(t, 2, u - 1, BLOCKS):
                    for k in range(EC):
                        wait_for(act, s_t2, t, 2 * EC, EC * (u - 1) + k + 1)
                        wait_for(act, s_h2lo, t, 2 * EC, EC * (u - 2) + k + 1)
                        act.activation(hf[:, k, :], pt[:, k, :], ACT.Identity, bias=affine[:, EC + k:EC + k + 1],
                                       scale=affine[:, k:k + 1]).then_inc(s_hf, 1)
                    for k in range(EC):
                        wait_for(act, s_hf, t, 2 * EC, EC * (u - 1) + k + 1)
                        wait_for(act, s_c, t, 4, 2 * (u - 1))
                        act.activation(h2T[:, 2 * k, :], hf[:, k, :], ACT.Copy).then_inc(s_h2hi, 1)

        def dve_window(dve, t, u):
            for s in range(FC):
                c = FC * u + s - 1
                if live(t, 2 * FC, c, CHUNKS):
                    wait_for(dve, s_gh, t, 2 * FC, c + 1)
                    wait_for(dve, s_y, t, 2 * FC, c - GR + 1)
                    dve.tensor_tensor(gl[:, c % GR, :], g[:, c % GR, :], gh[:, c % GR, :].bitcast(F32),
                                      ALU.subtract).then_inc(s_gl, 1)
                if s == 0 and live(t, 2, u + 1, BLOCKS):
                    norm.stats(dve, t, u + 1, lambda j: x_tile(t, u + 1, j))
                if s == 1 and live(t, 2, u + 1, BLOCKS):
                    norm.shifts(dve, t, u + 1)
                    wait_for(dve, s_t, t, 2 * EC, EC * (u + 1))
                    for j in range(BT):
                        norm.apply(dve, j, h[:, j, :], x_tile(t, u + 1, j)).then_inc(s_h, 1)
                if s == 1 and inner is not None and live(t, 2, u - 2, BLOCKS):
                    for which in range(2):
                        wait_for(dve, s_chi, t, 4, 2 * (u - 2) + which + 1)
                        dve.tensor_tensor(cT[:, 2 * which + 1, :], pt[:, which, :],
                                          cT[:, 2 * which, :].bitcast(F32), ALU.subtract).then_inc(s_clo, 1)
                if s == 3 and live(t, 2, u + 1, BLOCKS):
                    for k in range(EC):
                        wait_for(dve, s_hi, t, 2 * EC, EC * (u + 1) + k + 1)
                        dve.tensor_tensor(hT[:, (u + 1) % 2, 2 * k + 1, :], pt[:, k, :],
                                          hT[:, (u + 1) % 2, 2 * k, :].bitcast(F32), ALU.subtract).then_inc(s_lo, 1)
                if s == LAG and live(t, 2, u - 1, BLOCKS):
                    wait_for(dve, s_b, t, 2, u)
                    unit = 1 if out is None else 16
                    wait_for(dve, s_res, t, 2 * unit, unit * (u - 1))
                    wait_for(dve, s_y, t, 2 * FC, FC * u)
                    for j in range(BT):
                        dve.tensor_tensor(xnew[:, j, :], x_tile(t, u - 1, j), py[:, j, 0:E],
                                          ALU.add).then_inc(s_xa, 1)
                    if inner is not None:
                        wait_for(dve, s_xa, t, 2 * BT, BT * u)
                        norm_x.stats(dve, t, u - 1, lambda j: xnew[:, j, :])
                if inner is None or not live(t, 2, u - 1, BLOCKS):
                    continue
                if s == LAG + 1:
                    norm_x.shifts(dve, t, u - 1)
                    for j in range(BT):
                        norm_x.apply(dve, j, xn[:, j, :], xnew[:, j, :]).then_inc(s_xn, 1)
                    wait_for(dve, s_xn, t, 2 * BT, BT * u)
                    norm_h.stats(dve, t, u - 1, lambda j: xn[:, j, :])
                if s == LAG + 2:
                    norm_h.shifts(dve, t, u - 1)
                    wait_for(dve, s_t2, t, 2 * EC, EC * (u - 1))
                    for j in range(BT):
                        norm_h.apply(dve, j, h2[:, j, :], xn[:, j, :]).then_inc(s_h2, 1)
                if s == 7:
                    for k in range(EC):
                        wait_for(dve, s_h2hi, t, 2 * EC, EC * (u - 1) + k + 1)
                        dve.tensor_tensor(h2T[:, 2 * k + 1, :], hf[:, k, :], h2T[:, 2 * k, :].bitcast(F32),
                                          ALU.subtract).then_inc(s_h2lo, 1)

        def pool_window(pool, t, u):
            if live(t, 2, u + 1, BLOCKS):
                norm.power(pool, t, u + 1)
                wait_for(pool, s_h, t, 2 * BT, BT * (u + 2))
                xs = tile_of(x, t * 2 * BT + (u + 1) * BT, BT).rearrange("p (a b) -> p a b", b=E)
                pool.tensor_tensor(xs, xs, b2s[:].unsqueeze(1).to_broadcast([P, BT, E]), ALU.add).then_inc(s_b, 1)
            if live(t, 2, u - 1, BLOCKS):
                dst = x[:, bass.ds(t * 2 * BT + (u - 1) * BT, BT), :]
                if inner is not None:
                    norm_x.power(pool, t, u - 1)
                    norm_h.power(pool, t, u - 1)
                    wait_for(pool, s_xn, t, 2 * BT, BT * u)
                    pool.tensor_tensor(dst, xnew[:], xn[:], ALU.add).then_inc(s_res, 1)
                elif out is None:
                    wait_for(pool, s_xa, t, 2 * BT, BT * u)
                    pool.tensor_copy(dst, xnew[:]).then_inc(s_res, 1)

        def sp_window(sp, t, u):
            if out is not None and live(t, 2, u - 1, BLOCKS):
                tiles = out.rearrange("(n p) e -> p n e", p=P)
                wait_for(sp, s_xa, t, 2 * BT, BT * u)
                sp.dma_start(tiles[:, bass.ds(t * 2 * BT + (u - 1) * BT, BT), :], xnew[:]).then_inc(s_res, 16)
            if inner is not None and live(t, 2, u - 2, BLOCKS):
                wait_for(sp, s_clo, t, 4, 2 * (u - 1))
                store_block(sp, scratch, t, u - 2, cT[:], s_out)

        block = ctx.enter_context(nc.Block())

        @block.sync
        def _(sp):
            for src, dst in ((w1.rearrange("(c p) f -> p c f", p=P), w1r), (w2.rearrange("(c p) f -> p c f", p=P), w2r),
                             (b1, b1s), (b2.partition_broadcast(P), b2s)):
                sp.dma_start(dst[:], src).then_inc(s_w, 16)
            if inner is not None:
                sp.dma_start(wdr[:], w_down).then_inc(s_wd, 16)
                sp.dma_start(affine[:], ln_affine).then_inc(s_wd, 16)
            run_bodies(sp, sp_window, BLOCKS // 2, True)
            if out is not None:
                sp.wait_ge(s_res, 16 * BLOCKS)
            if inner is not None:
                sp_window(sp, BLOCKS // 2, 1)
                sp.wait_ge(s_out, 16 * BLOCKS)

        def halves(w):
            n = w.shape[1] // 2
            return [w[:, i * n:(i + 1) * n, :].rearrange("p a b -> p (a b)") for i in range(2)]

        @block.gpsimd
        def _(pool):
            pool.wait_ge(s_w, 64)
            if inner is not None:
                flat = lambda w: w[:].rearrange("p a b c -> p (a b c)")
                pool.wait_ge(s_wd, 32)
                pool_round(pool, flat(wdh), wdr[:], consts[0]).then_inc(s_wds, 1)
                pool.wait_ge(s_wds, 1)
                pool.tensor_tensor(flat(wdl), wdr[:], flat(wdh).bitcast(F32), ALU.subtract).then_inc(s_wds, 1)
            run_bodies(pool, pool_window, BLOCKS // 2, True)

        @block.scalar
        def _(act):
            act.wait_ge(s_w, 64)
            for hi, raw in ((w1h, w1r), (w2h, w2r)):
                for a, b in zip(halves(hi), halves(raw)):
                    act.activation(a, b, ACT.Copy).then_inc(s_whi, 1)
            if inner is not None:
                act.wait_ge(s_wd, 32)
            run_bodies(act, act_window, BLOCKS // 2, True)
            if inner is not None:
                act_window(act, BLOCKS // 2, 1)

        @block.vector
        def _(dve):
            dve.wait_ge(s_w, 64)
            n = 0
            for hi, lo, raw in ((w1h, w1l, w1r), (w2h, w2l, w2r)):
                for a, b, c in zip(halves(lo), halves(raw), halves(hi)):
                    n += 1
                    dve.wait_ge(s_whi, n)
                    dve.tensor_tensor(a, b, c.bitcast(F32), ALU.subtract).then_inc(s_wlo, 1)
            run_bodies(dve, dve_window, BLOCKS // 2, True)
            if inner is not None:
                dve_window(dve, BLOCKS // 2, 1)

        @block.tensor
        def _(pe):
            pe.wait_ge(s_wlo, 4)
            if inner is not None:
                pe.wait_ge(s_wds, 2)
            run_bodies(pe, pe_window, BLOCKS // 2, True)
            if inner is not None:
                pe_window(pe, BLOCKS // 2, 1)


def attention(nc, name, x, ident, zero, scratch, w_qk, w_v, w_out, scale, rope):
    with ExitStack() as ctx:
        sb = lambda n, shape, dt=F32: ctx.enter_context(nc.sbuf_tensor(f"{name}_{n}", shape, dt))
        psum = lambda n, shape: ctx.enter_context(nc.psum_tensor(f"{name}_{n}", shape, F32))
        sem = lambda n: ctx.enter_context(nc.semaphore(f"{name}_{n}"))
        WC, VC = w_qk.shape[2], w_v.shape[2]
        VW = 2 * P
        NQ = 8 if rope is not None else 4
        if rope is not None:
            unit_steps = {1: 0, 2: 1, 3: 2, 5: 3, 6: 4, 7: 5, 9: 6, 10: 7}
            v_steps = {11: 0, 13: 1, 14: 2, 15: 3}
            convert_steps = {3: 0, 6: 1, 8: 2, 11: 3}
        else:
            unit_steps = {1: 0, 2: 1, 3: 2, 5: 3}
            v_steps = {7: 0, 9: 1, 10: 2, 11: 3}
            convert_steps = {1: 0, 2: 1, 3: 2, 5: 3}

        hT = sb("hT", [P, 4, S], F32R)
        wraw, woraw = sb("wraw", [P, WC]), sb("woraw", [P, E])
        wh, wl = sb("wh", [P, 2, WC], F32R), sb("wl", [P, 2, WC], F32R)
        wvraw, wvh, wvl = sb("wvraw", [P, VC]), sb("wvh", [P, VC], F32R), sb("wvl", [P, VC], F32R)
        woh, wol = sb("woh", [P, 2, E], F32R), sb("wol", [P, 2, E], F32R)
        nat_h, nat_l = sb("nat_h", [P, 2, BLOCK], F32R), sb("nat_l", [P, 2, BLOCK], F32R)
        q_h = sb("q_h", [P, 2, 2, S], F32R)
        q_l = sb("q_l", [P, 2, 2, S], F32R)
        k_s = sb("k_s", [P, 2, 2, S], F32R)
        v = sb("v", [P, 2, KT, P])
        v_next = sb("v_next", [P, KT, P])
        p = sb("p", [P, PRING, S])
        pT = sb("pT", [P, 2, 2, KT, GW])
        nmax = sb("nmax", [P, NM])
        rsum, rinv = sb("rsum", [P, NM]), sb("rinv", [P, NM])
        o_h, o_l = sb("o_h", [P, 2, GW], F32R), sb("o_l", [P, 2, GW], F32R)
        if rope is not None:
            cos_t, sin_t = sb("cos_t", [P, S]), sb("sin_t", [P, S])
            rot_a, rot_b, rot = sb("rot_a", [P, BLOCK]), sb("rot_b", [P, BLOCK]), sb("rot", [P, BLOCK])

        ps_s = psum("ps_s", [P, 2, S])
        ps_t = psum("ps_t", [P, 2, 4, P])
        ps_o = psum("ps_o", [P, BLOCK])
        ps_m = psum("ps_m", [P, BLOCK])

        s_ht, s_raw, s_rawo = sem("s_ht"), sem("s_raw"), sem("s_rawo")
        s_rope = sem("s_rope")
        s_wsplit, s_wosplit = sem("s_wsplit"), sem("s_wosplit")
        s_proj, s_rot, s_rr, s_nat = sem("s_proj"), sem("s_rot"), sem("s_rr"), sem("s_nat")
        s_rawv, s_wvsplit = sem("s_rawv"), sem("s_wvsplit")
        s_vp, s_v, s_vmove = sem("s_vp"), sem("s_v"), sem("s_vmove")
        s_stack = [sem("s_stack0"), sem("s_stack1")]
        s_scores, s_max, s_exp, s_tr, s_tev = (sem(n) for n in ("s_scores", "s_max", "s_exp", "s_tr", "s_tev"))
        s_recip, s_norm, s_pv, s_oh, s_ol = (sem(n) for n in ("s_recip", "s_norm", "s_pv", "s_oh", "s_ol"))
        s_wo, s_x = sem("s_wo"), sem("s_x")
        QD, KD = 8, 4
        SD = 16 * (QD + KD)

        VMOVE = 8
        def users(t, u):
            for s in range(STEPS):
                c = STEPS * u + s
                if s % GS == 0:
                    g = (c - WO_LAG) // GS
                    if live(t, 2 * PG, g, NGROUP):
                        yield s, (s_x, 2 * PG, g + 1)
                elif s in unit_steps and live(t, 2, u + 1, NPAIR):
                    j = unit_steps[s]
                    if rope is not None:
                        yield s, (s_rot, 2 * NQ, NQ * (u + 1) + j + 1)
                    else:
                        yield s, (s_nat, 2 * 8, 8 * (u + 1) + 2 * j + 2)
                elif u == 1 and s in v_steps and live(t, 1, 1, BODIES):
                    yield s, (s_v, 8, 8 + 2 * v_steps[s] + 2)

        def wait_ps_m(pe, t, u, s):
            last = None
            for at, (sm, per_body, c) in users(t, u):
                if at >= s:
                    break
                last = (sm, per_body, c)
            if last is None:
                tt, uu = (t, 0) if u == 1 else (t - 1, 1)
                for at, (sm, per_body, c) in users(tt, uu):
                    last = (sm, per_body, c if u == 1 else c - per_body)
            if last is not None:
                wait_for(pe, last[0], t, last[1], last[2])

        def scores(pe, t, c):
            par, buf, cc = (c // STEPS) % 2, c % 2, c % STEPS
            head, qt = (cc % GS) // GQ, GQ * (cc // GS) + cc % GQ
            if cc == 0:
                pair = c // STEPS
                for s in s_stack:
                    wait_for(pe, s, t, 2 * SD, SD * (pair + 1))
            wait_for(pe, s_exp, t, 2 * STEPS, c - 1)
            cols = slice(qt * P, (qt + 1) * P)
            for first, q in ((True, q_h), (False, q_l)):
                for kh in range(HALVES):
                    keys = slice(kh * BLOCK, (kh + 1) * BLOCK)
                    mm = pe.matmul(ps_s[:, buf, keys], q[:, par, head, cols], k_s[:, par, head, keys],
                                   start=first, stop=not first)
            mm.then_inc(s_scores, 1)

        def transposes(pe, t, c):
            wait_for(pe, s_norm, t, 2 * STEPS, c + 1)
            for h in range(2):
                wait_for(pe, s_tev, t, 4 * STEPS, 2 * c + h - 1)
                for k in range(4):
                    kt = 4 * h + k
                    mm = pe.transpose(ps_t[:, h, k, :], p[:, c % PRING, kt * P:(kt + 1) * P], ident[:])
                mm.then_inc(s_tr, 1)

        def pv(pe, t, g, j):
            pair = g // PG
            if j == 0:
                wait_for(pe, s_tev, t, 4 * STEPS, 2 * GS * (g + 1))
                wait_for(pe, s_ol, t, 2 * PG, g)
                if pair % 2 == 0:
                    wait_for(pe, s_v, t, 8, 8 * (pair // 2 + 1))
                else:
                    wait_for(pe, s_vmove, t, 1, pair // 2 + 1)
            for kt in range(2 * j, 2 * j + 2):
                for head in range(2):
                    rows = slice(D * head, D * (head + 1))
                    mm = pe.matmul(ps_o[rows, 0:GW], v[:, pair % 2, kt, rows], pT[:, g % 2, head, kt, :],
                                   start=kt == 0, stop=kt == KT - 1)
            if j == GS - 1:
                mm.then_inc(s_pv, 1)

        def out_project(pe, t, u, s, g):
            wait_for(pe, s_ol, t, 2 * PG, g + 1)
            wait_for(pe, s_wosplit, t, 4, 2 * (g // PG + 1))
            wait_ps_m(pe, t, u, s)
            par = (g // PG) % 2
            for qi in range(GQ):
                rows = slice(qi * P, (qi + 1) * P)
                for n, (o, w) in enumerate(((o_h, woh), (o_h, wol), (o_l, woh))):
                    mm = pe.matmul(ps_m[:, qi * E:(qi + 1) * E], o[:, g % 2, rows], w[:, par, :],
                                   start=n == 0, stop=n == 2)
            mm.then_inc(s_wo, 1)

        def project_qk(pe, t, u, s, j):
            pair = u + 1
            if j == 0:
                wait_for(pe, s_ht, t, 16, 16 * (pair // 2 + 1))
                wait_for(pe, s_wsplit, t, 4, 2 * (pair + 1))
            wait_ps_m(pe, t, u, s)
            par = pair % 2
            if rope is not None:
                which, half, variant = j // 4, (j // 2) % 2, j % 2
                blocks = [(2 * which + variant, 2 * which)]
            else:
                which, half = j // 2, j % 2
                blocks = [(2 * which + c, 2 * c) for c in range(EC)]
            cols = slice(half * BLOCK, (half + 1) * BLOCK)
            prods = [(wb, fb, w, f) for wb, fb in blocks for w, f in ((wh, 0), (wh, 1), (wl, 0))]
            for n, (wb, fb, w, f) in enumerate(prods):
                mm = pe.matmul(ps_m[:, :], w[:, par, wb * P:(wb + 1) * P], hT[:, fb + f, cols],
                               start=n == 0, stop=n == len(prods) - 1)
            mm.then_inc(s_proj, 1)

        def project_v(pe, t, u, s, j):
            if j == 0:
                wait_for(pe, s_wvsplit, t, 2, 2 * 2)
            wait_ps_m(pe, t, u, s)
            blocks = [(0, 2)] if rope is not None else [(c, 2 * c) for c in range(EC)]
            prods = [(wb, fb, w, f) for wb, fb in blocks for w, f in ((wvh, 0), (wvh, 1), (wvl, 0))]
            for i in range(2):
                kt = 2 * j + i
                for n, (wb, fb, w, f) in enumerate(prods):
                    mm = pe.matmul(ps_m[:, i * VW:(i + 1) * VW], hT[:, fb + f, kt * P:(kt + 1) * P],
                                   w[:, wb * VW:(wb + 1) * VW], start=n == 0, stop=n == len(prods) - 1)
            mm.then_inc(s_vp, 1)

        def pe_window(pe, t, u):
            for s in range(STEPS):
                c = STEPS * u + s
                if live(t, 2 * STEPS, c, NSTEP):
                    scores(pe, t, c)
                if live(t, 2 * STEPS, c - T_LAG, NSTEP):
                    transposes(pe, t, c - T_LAG)
                g = (c - WO_LAG) // GS
                if s % GS == 0 and live(t, 2 * PG, g, NGROUP):
                    out_project(pe, t, u, s, g)
                if s in unit_steps and live(t, 2, u + 1, NPAIR):
                    project_qk(pe, t, u, s, unit_steps[s])
                if u == 1 and s in v_steps and live(t, 1, 1, BODIES):
                    project_v(pe, t, u, s, v_steps[s])
                g, j = (c - PV_LAG) // GS, (c - PV_LAG) % GS
                if live(t, 2 * PG, g, NGROUP):
                    pv(pe, t, g, j)

        def convert(dve, t, u, jj, src):
            pair, which, half = u + 1, jj // 2, jj % 2
            wait_for(dve, s_stack[half], t, 2 * SD, SD * pair + (16 * QD if which else 0))
            mul = scale if which == 0 else 1.0
            dve.tensor_scalar(nat_h[:, half, :], src, mul, None, ALU.mult).then_inc(s_nat, 1)
            wait_for(dve, s_nat, t, 16, 8 * pair + 2 * jj + 1)
            dve.scalar_tensor_tensor(nat_l[:, half, :], src, mul, nat_h[:, half, :].bitcast(F32),
                                     ALU.mult, ALU.subtract).then_inc(s_nat, 1)

        def dve_window(dve, t, u):
            for s in range(STEPS):
                c = STEPS * u + s
                g = (c - O_LAG) // GS
                if c % GS == O_LAG % GS and live(t, 2 * PG, g, NGROUP):
                    wait_for(dve, s_oh, t, 2 * PG, g + 1)
                    dve.tensor_tensor(o_l[:, g % 2, :], ps_o[:, 0:GW], o_h[:, g % 2, :].bitcast(F32),
                                      ALU.subtract).then_inc(s_ol, 1)
                n = c - N_LAG
                if live(t, 2 * STEPS, n, NSTEP):
                    wait_for(dve, s_exp, t, 2 * STEPS, n + 1)
                    wait_for(dve, s_norm, t, 2 * STEPS, n - NM + 1)
                    dve.reciprocal(rinv[:, n % NM:n % NM + 1], rsum[:, n % NM:n % NM + 1]).then_inc(s_recip, 1)
                if live(t, 2 * STEPS, c, NSTEP):
                    wait_for(dve, s_scores, t, 2 * STEPS, c + 1)
                    dve.reduce_max(nmax[:, c % NM:c % NM + 1], ps_s[:, c % 2, :], AX_X,
                                   negate=True).then_inc(s_max, 1)
                if live(t, 2 * STEPS, n, NSTEP):
                    wait_for(dve, s_recip, t, 2 * STEPS, n + 1)
                    dve.tensor_scalar(p[:, n % PRING, :], p[:, n % PRING, :], rinv[:, n % NM:n % NM + 1], None,
                                      ALU.mult).then_inc(s_norm, 1)
                if u == 0 and s == VMOVE and live(t, 1, 0, BODIES):
                    wait_for(dve, s_pv, t, 2 * PG, 0)
                    wait_for(dve, s_v, t, 8, 8)
                    dve.tensor_copy(v[:, 1, :, :], v_next[:]).then_inc(s_vmove, 1)
                if s in convert_steps and rope is not None and live(t, 2, u + 1, NPAIR):
                    jj = convert_steps[s]
                    wait_for(dve, s_rr, t, 8, 4 * (u + 1) + jj + 1)
                    convert(dve, t, u, jj, rot[:])
                if s in unit_steps and live(t, 2, u + 1, NPAIR):
                    j = unit_steps[s]
                    wait_for(dve, s_proj, t, 2 * NQ, NQ * (u + 1) + j + 1)
                    if rope is None:
                        convert(dve, t, u, j, ps_m[:, :])
                    else:
                        half, variant = (j // 2) % 2, j % 2
                        wait_for(dve, s_rr, t, 8, 4 * (u + 1) + j // 2)
                        cols = slice(half * BLOCK, (half + 1) * BLOCK)
                        dve.tensor_tensor((rot_b if variant else rot_a)[:], ps_m[:, :],
                                          (sin_t if variant else cos_t)[:, cols], ALU.mult).then_inc(s_rot, 1)
                if u == 1 and s in v_steps and live(t, 1, 1, BODIES):
                    j = v_steps[s]
                    wait_for(dve, s_vp, t, 4, 4 + j + 1)
                    src = ps_m[:, :].rearrange("p (a b) -> p a b", b=VW)
                    wait_for(dve, s_pv, t, 2 * PG, PG)
                    dve.tensor_copy(v[:, 0, 2 * j:2 * j + 2, :], src[:, :, 0:P]).then_inc(s_v, 1)
                    wait_for(dve, s_vmove, t, 1, 1)
                    dve.tensor_copy(v_next[:, 2 * j:2 * j + 2, :], src[:, :, P:VW]).then_inc(s_v, 1)
                g = (c - WO_LAG) // GS
                if s % GS == 0 and live(t, 2 * PG, g, NGROUP):
                    wait_for(dve, s_wo, t, 2 * PG, g + 1)
                    body = t if g >= 0 else t - 1
                    tile = (body // (PAIRS // 2)) * KT + GQ * (g % PG)
                    xs = tile_of(x, tile, GQ)
                    dve.tensor_tensor(xs, xs, ps_m[:, :], ALU.add).then_inc(s_x, 1)

        def act_window(act, t, u):
            for s in range(STEPS):
                c = STEPS * u + s
                g = (c - O_LAG) // GS
                if c % GS == O_LAG % GS and live(t, 2 * PG, g, NGROUP):
                    wait_for(act, s_pv, t, 2 * PG, g + 1)
                    wait_for(act, s_wo, t, 2 * PG, g - 1)
                    act.activation(o_h[:, g % 2, :], ps_o[:, 0:GW], ACT.Copy).then_inc(s_oh, 1)
                b = c - T_LAG
                if live(t, 2 * STEPS, b, NSTEP):
                    g, head, qi = b // GS, (b % GS) // GQ, b % GQ
                    for h in range(2):
                        wait_for(act, s_tr, t, 4 * STEPS, 2 * b + h + 1)
                        if b % GS == 0 and h == 0:
                            wait_for(act, s_pv, t, 2 * PG, g - 1)
                        act.activation(pT[:, g % 2, head, 4 * h:4 * h + 4, qi * P:(qi + 1) * P],
                                       ps_t[:, h, :, :], ACT.Copy).then_inc(s_tev, 1)
                if live(t, 2 * STEPS, c, NSTEP):
                    wait_for(act, s_max, t, 2 * STEPS, c + 1)
                    wait_for(act, s_tr, t, 4 * STEPS, 2 * (c - PRING) + 2)
                    act.activation(p[:, c % PRING, :], ps_s[:, c % 2, :], ACT.Exp,
                                   bias=nmax[:, c % NM:c % NM + 1],
                                   accum_out=rsum[:, c % NM:c % NM + 1]).then_inc(s_exp, 1)

        def split_qk(pool, t, par, pair):
            wait_for(pool, s_raw, t, 32, 16 * (pair + 1))
            wait_for(pool, s_proj, t, 2 * NQ, NQ * (pair - 1))
            pool_round(pool, wh[:, par, :], wraw[:], zero).then_inc(s_wsplit, 1)
            wait_for(pool, s_wsplit, t, 4, 2 * pair + 1)
            pool.tensor_tensor(wl[:, par, :], wraw[:], wh[:, par, :].bitcast(F32),
                               ALU.subtract).then_inc(s_wsplit, 1)

        def split_v(pool, t, body):
            wait_for(pool, s_rawv, t, 16, 16 * (body + 1))
            wait_for(pool, s_vp, t, 4, 4 * body)
            pool_round(pool, wvh[:], wvraw[:], zero).then_inc(s_wvsplit, 1)
            wait_for(pool, s_wvsplit, t, 2, 2 * body + 1)
            pool.tensor_tensor(wvl[:], wvraw[:], wvh[:].bitcast(F32), ALU.subtract).then_inc(s_wvsplit, 1)

        def pool_window(pool, t, u):
            for s in range(STEPS):
                c = STEPS * u + s
                if rope is not None and s in unit_steps and unit_steps[s] % 2 and live(t, 2, u + 1, NPAIR):
                    jj = unit_steps[s] // 2
                    wait_for(pool, s_rot, t, 2 * NQ, NQ * (u + 1) + 2 * jj + 2)
                    wait_for(pool, s_nat, t, 16, 8 * (u + 1) + 2 * jj)
                    pool.tensor_tensor(rot[:], rot_a[:], rot_b[:], ALU.add).then_inc(s_rr, 1)
                if s == 7 and u == 0 and live(t, 1, 1, BODIES):
                    split_v(pool, t, 1)
                if s == 3 and live(t, 2, u + 2, NPAIR):
                    split_qk(pool, t, u, u + 2)
                if s == 11 and live(t, 2, u + 1, NPAIR):
                    pair = u + 1
                    wait_for(pool, s_rawo, t, 32, 16 * (pair + 1))
                    wait_for(pool, s_wo, t, 2 * PG, PG * (pair - 1))
                    pool_round(pool, woh[:, pair % 2, :], woraw[:], zero).then_inc(s_wosplit, 1)
                    wait_for(pool, s_wosplit, t, 4, 2 * pair + 1)
                    pool.tensor_tensor(wol[:, pair % 2, :], woraw[:], woh[:, pair % 2, :].bitcast(F32),
                                       ALU.subtract).then_inc(s_wosplit, 1)

        def pair_of_batch(t, pair):
            return ((t + pair // 2) % (PAIRS // 2)) * 2 + pair % 2

        def sp_window(sp, t, u):
            if live(t, 2, u + 2, NPAIR):
                source = pair_of_batch(t, u + 2)
                wait_for(sp, s_wsplit, t, 4, 2 * (u + 2))
                sp.dma_start(wraw[:], w_qk[source]).then_inc(s_raw, 16)
            if u == 0 and live(t, 1, 1, BODIES):
                source = (t + 1) % (PAIRS // 2)
                wait_for(sp, s_wvsplit, t, 2, 2)
                sp.dma_start(wvraw[:], w_v[source]).then_inc(s_rawv, 16)
            if live(t, 2, u + 1, NPAIR):
                pair = u + 1
                par = pair % 2
                source = pair_of_batch(t, pair)
                wait_for(sp, s_wosplit, t, 4, 2 * pair)
                sp.dma_start(woraw[:], w_out[source]).then_inc(s_rawo, 16)
                for jj in range(4):
                    which, half = jj // 2, jj % 2
                    cols = slice(half * BLOCK, (half + 1) * BLOCK)
                    wait_for(sp, s_nat, t, 16, 8 * pair + 2 * jj + 2)
                    parts = [(q_h, nat_h, nat_h), (q_l, nat_l, nat_l)] if which == 0 else [(k_s, nat_h, nat_l)]
                    for dst, top, bottom in parts:
                        for head in range(2):
                            rows = slice(D * head, D * (head + 1))
                            for r, src in ((0, top), (D, bottom)):
                                sp.dma_start(dst[r:r + D, par, head, cols].bitcast(F32),
                                             src[rows, half, :].bitcast(F32)).then_inc(s_stack[half], 16)
            if u == 0 and live(t, 1, 1, BODIES):
                source = (t + 1) // (PAIRS // 2)
                wait_for(sp, s_proj, t, 2 * NQ, 2 * NQ)
                sp.dma_start(hT[:].bitcast(F32), scratch[source].bitcast(F32)).then_inc(s_ht, 16)

        block = ctx.enter_context(nc.Block())

        @block.sync
        def _(sp):
            sp.dma_start(hT[:].bitcast(F32), scratch[0].bitcast(F32)).then_inc(s_ht, 16)
            sp.dma_start(wraw[:], w_qk[0]).then_inc(s_raw, 16)
            sp.dma_start(wvraw[:], w_v[0]).then_inc(s_rawv, 16)
            if rope is not None:
                sp.dma_start(cos_t[:], rope[0]).then_inc(s_rope, 16)
                sp.dma_start(sin_t[:], rope[1]).then_inc(s_rope, 16)
            run_bodies(sp, sp_window, BODIES, True)

        @block.gpsimd
        def _(pool):
            split_qk(pool, 0, 0, 0)
            split_v(pool, 0, 0)
            run_bodies(pool, pool_window, BODIES, True)

        @block.vector
        def _(dve):
            if rope is not None:
                dve.wait_ge(s_rope, 32)
            run_bodies(dve, dve_window, BODIES, True)

        @block.scalar
        def _(act):
            run_bodies(act, act_window, BODIES, True)

        @block.tensor
        def _(pe):
            run_bodies(pe, pe_window, BODIES, True)


def hybrid_stack(nc, x_in, wa_qk, wa_v, wa_out, wb_down, ln_affine, wb_qk, wb_v, wb_out, rope, w1, b1, w2, b2, out):
    feat_a = nc.dram_tensor("feat_a", [B, P, 4, S], F32R).ap()
    feat_b = nc.dram_tensor("feat_b", [B, P, 4, S], F32R).ap()
    with ExitStack() as ctx:
        x = ctx.enter_context(nc.sbuf_tensor("x", [P, TILES, E], F32))
        ident = ctx.enter_context(nc.sbuf_tensor("ident", [P, P], F32))
        zero, eps, minus_half = (ctx.enter_context(nc.sbuf_tensor(n, [P, 1], F32))
                                 for n in ("zero", "eps", "minus_half"))
        s_id = ctx.enter_context(nc.semaphore("s_id"))
        with nc.Block() as block:
            @block.gpsimd
            def _(pool):
                pool.memset(ident[:], 0.0).then_inc(s_id, 1)
                pool.wait_ge(s_id, 1)
                pool.affine_select(out=ident[:], in_=ident[:], compare_op=ALU.not_equal, fill=1.0, base=0,
                                   pattern=[[-1, P]], channel_multiplier=1).then_inc(s_id, 1)
                for tile, value in ((zero, 0.0), (eps, EPS), (minus_half, -0.5)):
                    pool.memset(tile[:], value).then_inc(s_id, 1)
                pool.wait_ge(s_id, 5)

        consts = (zero, eps, minus_half)
        features_a(nc, x_in, x, ident, consts, feat_a)
        attention(nc, "a", x, ident, zero, feat_a, wa_qk, wa_v, wa_out, 1.0 / (D * D * H), None)
        ffn(nc, "f1", x, ident, consts, w1, b1, w2, b2, inner=(wb_down, ln_affine, feat_b))
        attention(nc, "b", x, ident, zero, feat_b, wb_qk, wb_v, wb_out, 1.0 / D ** 0.5, rope)
        ffn(nc, "f2", x, ident, consts, w1, b1, w2, b2, out=out)


def rope_tables():
    inv_freq = 1.0 / 10000.0 ** (np.arange(0, D, 2, dtype=np.float32) / D)
    freqs = np.outer(np.arange(S, dtype=np.float32), inv_freq)
    cos = np.concatenate([np.cos(freqs), np.cos(freqs)], -1)[:, ::2]
    sin = np.concatenate([np.sin(freqs), np.sin(freqs)], -1)[:, ::2]
    rows = np.arange(P)
    sign = np.where(rows % 2 == 0, -1.0, 1.0).astype(np.float32)
    pick = (rows % D) // 2
    return np.ascontiguousarray(np.stack([cos.T[pick], sin.T[pick] * sign[:, None]]).astype(np.float32))


def kernel(**inputs):
    import concourse.bacc as bacc
    from concourse.bass_utils import run_bass_kernel_spmd

    g = {k: np.asarray(v) for k, v in inputs.items()}
    ka = g["L0_attn_a_kernel"].reshape(3, PAIRS, 2, EC, P, D)
    wa_qk = ka[:2].transpose(1, 4, 0, 3, 2, 5).reshape(PAIRS, P, 2 * EC * P)
    wa_v = ka[2].reshape(PAIRS // 2, 4, EC, P, D).transpose(0, 3, 2, 1, 4).reshape(PAIRS // 2, P, EC * 2 * P)
    wa_out = g["L0_attn_a_WO"][0].reshape(D, PAIRS, 2, E).transpose(1, 2, 0, 3).reshape(PAIRS, P, E)
    up = {n: g["L0_attn_b_w_up_" + n].reshape(PAIRS, P, P) for n in "qkv"}
    partner = np.arange(P) ^ 1
    blocks = [up["q"], up["q"][:, partner], up["k"], up["k"][:, partner]]
    wb_qk = np.stack(blocks, 1).transpose(0, 3, 1, 2).reshape(PAIRS, P, 4 * P)
    wb_v = up["v"].reshape(PAIRS // 2, 2 * P, P).transpose(0, 2, 1)
    wb_out = g["L0_attn_b_w_out"].T.reshape(PAIRS, P, E)
    down = np.stack([g["L0_attn_b_w_down_q"], g["L0_attn_b_w_down_kv"]])
    wb_down = down.reshape(2, P, EC, P).transpose(3, 2, 0, 1).reshape(P, EC * 2 * P)
    ln_affine = np.stack([g["L0_attn_b_ln_scale"], g["L0_attn_b_ln_bias"]]).reshape(2 * EC, P).T
    arrays = {
        "x_in": g["L0_attn_a_x"].reshape(B * S, E), "wa_qk": wa_qk, "wa_v": wa_v, "wa_out": wa_out,
        "wb_down": wb_down, "ln_affine": ln_affine, "wb_qk": wb_qk, "wb_v": wb_v, "wb_out": wb_out,
        "rope": rope_tables(), "w1": g["L0_ffn_w1"], "b1": g["L0_ffn_b1"].reshape(FC, P).T,
        "w2": g["L0_ffn_w2"], "b2": g["L0_ffn_b2"],
    }
    arrays = {k: np.ascontiguousarray(a) for k, a in arrays.items()}
    nc = bacc.Bacc("TRN2", target_bir_lowering=False, num_devices=1)
    aps = {k: nc.dram_tensor(k, a.shape, mybir.dt.from_np(a.dtype), kind="ExternalInput").ap()
           for k, a in arrays.items()}
    out = nc.dram_tensor("out", (B * S, E), F32, kind="ExternalOutput").ap()
    hybrid_stack(nc, out=out, **aps)
    r = run_bass_kernel_spmd(nc, [arrays], core_ids=[0])
    return r.results[0]["out"].reshape(B, S, E)
```

```python
from contextlib import ExitStack

import numpy as np

import concourse.bass as bass
from concourse import mybir

F32 = mybir.dt.float32
F32R = mybir.dt.float32r
ACT = mybir.ActivationFunctionType
ALU = mybir.AluOpType
AX_X = mybir.AxisListType.X

P = 128
B, S, E = 4, 1024, 256
H, D = 16, 64
FF = 1024
TILES = B * S // P
BLOCK = 512
BLOCKS = B * S // BLOCK
BT = BLOCK // P
EC = E // P
FC = FF // P
KT = S // P
HALVES = S // BLOCK
EPS = 1e-5

PAIRS = H // 2
NPAIR = B * PAIRS
STEPS = 2 * KT
NSTEP = NPAIR * STEPS
GQ = 2
GW = GQ * P
GS = 2 * GQ
PG = STEPS // GS
NGROUP = NPAIR * PG
BODIES = NPAIR // 2
PRING = 4
NM = 4
N_LAG, T_LAG, PV_LAG, O_LAG, WO_LAG = 2, 3, 7, 11, 12
assert B % 2 == 0 and PAIRS % 2 == 0 and PG == 4 and GS == 4


def wait(eng, sem, value):
    if not isinstance(value, int) or value > 0:
        eng.wait_ge(sem, value)


def live(t, per_body, c, total):
    return not isinstance(t, int) or 0 <= per_body * t + c < total


def wait_for(eng, sem, t, per_body, c):
    wait(eng, sem, t * per_body + c)


def tile_of(tensor, index, count=1):
    return tensor[:, bass.ds(index, count), :].rearrange("p a b -> p (a b)")


def pool_round(pool, hi, src, zero):
    return pool.tensor_tensor(hi, src, zero[:].to_broadcast(list(src.shape)), ALU.add)


def split3(w_hi, w_lo):
    return (w_hi, 0), (w_lo, 0), (w_hi, 1)


class BlockNorm:

    def __init__(self, nc, ctx, name, consts):
        sb = lambda n, shape: ctx.enter_context(nc.sbuf_tensor(f"{name}_{n}", shape, F32))
        sem = lambda n: ctx.enter_context(nc.semaphore(f"{name}_{n}"))
        self.consts = consts
        self.parts = sb("parts", [P, BT, 2, 3])
        self.both, self.diff, self.sq = sb("both", [P, BT, 3]), sb("diff", [P, BT]), sb("sq", [P, BT])
        self.var = sb("var", [P, BT])
        self.ve, self.rstd, self.shift = sb("ve", [P, BT]), sb("rstd", [P, BT]), sb("shift", [P, BT])
        self.s_stats, self.s_rstd, self.s_shift = sem("s_stats"), sem("s_rstd"), sem("s_shift")
        self.s_var = sem("s_var")

    def stats(self, dve, t, c, src):
        for j in range(BT):
            dve.bn_stats(self.parts[:, j, :, :].rearrange("p a b -> p (a b)"), src(j)).then_inc(self.s_stats, 1)
        even, odd = self.parts[:, :, 0, :], self.parts[:, :, 1, :]
        wait_for(dve, self.s_stats, t, 2 * BT, BT * (c + 1))
        dve.tensor_tensor(self.diff[:], even[:, :, 1], odd[:, :, 1], ALU.subtract).then_inc(self.s_var, 1)
        dve.tensor_tensor(self.both[:], even, odd, ALU.add).then_inc(self.s_var, 1)
        wait_for(dve, self.s_var, t, 8, 4 * c + 1)
        dve.scalar_tensor_tensor(self.sq[:], self.diff[:], 0.25, self.diff[:],
                                 ALU.mult, ALU.mult).then_inc(self.s_var, 1)
        wait_for(dve, self.s_var, t, 8, 4 * c + 3)
        dve.scalar_tensor_tensor(self.var[:], self.both[:, :, 2], 1.0 / E, self.sq[:],
                                 ALU.mult, ALU.add).then_inc(self.s_var, 1)

    def power(self, pool, t, c):
        zero, eps, minus_half = self.consts
        wait_for(pool, self.s_var, t, 8, 4 * (c + 1))
        pool.tensor_tensor(self.ve[:], self.var[:], eps[:].to_broadcast([P, BT]), ALU.add).then_inc(self.s_rstd, 1)
        wait_for(pool, self.s_rstd, t, 4, 2 * c + 1)
        pool.tensor_tensor(self.rstd[:], self.ve[:], minus_half[:].to_broadcast([P, BT]), ALU.pow).then_inc(self.s_rstd, 1)

    def shifts(self, dve, t, c):
        wait_for(dve, self.s_rstd, t, 4, 2 * c + 2)
        dve.scalar_tensor_tensor(self.shift[:], self.both[:, :, 1], -0.5, self.rstd[:],
                                 ALU.mult, ALU.mult).then_inc(self.s_shift, 1)
        wait_for(dve, self.s_shift, t, 2, c + 1)

    def apply(self, dve, j, dst, src):
        return dve.tensor_scalar(dst, src, self.rstd[:, j:j + 1], self.shift[:, j:j + 1], ALU.mult, ALU.add)


def run_bodies(eng, window, bodies, ahead):
    if ahead:
        window(eng, -1, 1)
    for u in range(2):
        window(eng, 0, u)
    with eng.Fori(1, bodies - 1) as t:
        for u in range(2):
            window(eng, t, u)
    for u in range(2):
        window(eng, bodies - 1, u)
    window(eng, bodies, 0)


def transpose_block(pe, dst, h, ident, done):
    for c in range(EC):
        for j in range(BT):
            mm = pe.transpose(dst[:, c, j * P:(j + 1) * P], h[:, j, c * P:(c + 1) * P], ident[:])
        mm.then_inc(done, 1)


def store_block(eng, scratch, t, c, src, done):
    u = c % 2
    eng.dma_start(scratch[t + c // 2, :, :, u * BLOCK:(u + 1) * BLOCK].bitcast(F32),
                 src.bitcast(F32)).then_inc(done, 16)


def load_ahead(sp, scratch, ahead):
    feat, s_feat = ahead
    sp.dma_start(feat[:].bitcast(F32), scratch[0].bitcast(F32)).then_inc(s_feat, 16)


def features_a(nc, x_in, x, ident, consts, scratch, ahead):
    with ExitStack() as ctx:
        sb = lambda n, shape, dt=F32: ctx.enter_context(nc.sbuf_tensor(f"fa_{n}", shape, dt))
        sem = lambda n: ctx.enter_context(nc.semaphore(f"fa_{n}"))
        norm = BlockNorm(nc, ctx, "fa_n", consts)
        h = sb("h", [P, 2, BT, E])
        hT = sb("hT", [P, 2, 2 * EC, BLOCK], F32R)
        ps = ctx.enter_context(nc.psum_tensor("fa_ps", [P, 2, EC, BLOCK], F32))
        s_x, s_out = [sem("s_x0"), sem("s_x1")], [sem("s_out0"), sem("s_out1")]
        s_h, s_t, s_hi, s_lo = sem("s_h"), sem("s_t"), sem("s_hi"), sem("s_lo")
        tiles = x_in.rearrange("(n p) e -> p n e", p=P)

        def dve_window(dve, t, u):
            if live(t, 2, u, BLOCKS):
                wait_for(dve, s_x[u], t, 16, 16)
                dve.tensor_copy(h[:, u, :, :], x[:, bass.ds(t * 2 * BT + u * BT, BT), :]).then_inc(s_h, 1)
                wait_for(dve, s_h, t, 2 * (BT + 1), (BT + 1) * u + 1)
                norm.stats(dve, t, u, lambda j: h[:, u, j, :])
            if live(t, 2, u - 1, BLOCKS):
                lo(dve, t, u - 1)
            if live(t, 2, u, BLOCKS):
                norm.shifts(dve, t, u)
                for j in range(BT):
                    norm.apply(dve, j, h[:, u, j, :], h[:, u, j, :]).then_inc(s_h, 1)

        def lo(dve, t, c):
            for k in range(EC):
                wait_for(dve, s_hi, t, 2 * EC, EC * c + k + 1)
                dve.tensor_tensor(hT[:, c % 2, 2 * k + 1, :], ps[:, c % 2, k, :],
                                  hT[:, c % 2, 2 * k, :].bitcast(F32), ALU.subtract).then_inc(s_lo, 1)

        def pool_window(pool, t, u):
            if live(t, 2, u, BLOCKS):
                norm.power(pool, t, u)

        def pe_window(pe, t, u):
            if live(t, 2, u, BLOCKS):
                wait_for(pe, s_h, t, 2 * (BT + 1), (BT + 1) * (u + 1))
                wait_for(pe, s_lo, t, 2 * EC, EC * (u - 1))
                transpose_block(pe, ps[:, u, :, :], h[:, u, :, :], ident, s_t)

        def act_window(act, t, u):
            if live(t, 2, u, BLOCKS):
                wait_for(act, s_out[u], t, 16, 0)
                for k in range(EC):
                    wait_for(act, s_t, t, 2 * EC, EC * u + k + 1)
                    act.activation(hT[:, u, 2 * k, :], ps[:, u, k, :], ACT.Copy).then_inc(s_hi, 1)
            if live(t, 2, u - 1, BLOCKS):
                wait_for(act, s_lo, t, 2 * EC, EC * u)
                store_block(act, scratch, t, u - 1, hT[:, (u - 1) % 2, :, :], s_out[(u - 1) % 2])

        def sp_window(sp, t, u):
            if live(t, 2, u, BLOCKS):
                wait_for(sp, s_x[u], t, 16, 0)
                sp.dma_start(x[:, bass.ds(t * 2 * BT + u * BT, BT), :],
                             tiles[:, bass.ds(t * 2 * BT + u * BT, BT), :]).then_inc(s_x[u], 16)

        block = ctx.enter_context(nc.Block())

        @block.sync
        def _(sp):
            run_bodies(sp, sp_window, BLOCKS // 2, False)
            for s in s_out:
                sp.wait_ge(s, 16)
            load_ahead(sp, scratch, ahead)

        @block.gpsimd
        def _(pool):
            run_bodies(pool, pool_window, BLOCKS // 2, False)

        @block.vector
        def _(dve):
            run_bodies(dve, dve_window, BLOCKS // 2, False)

        @block.scalar
        def _(act):
            run_bodies(act, act_window, BLOCKS // 2, False)
            for s in s_out:
                act.wait_ge(s, 16 * BLOCKS // 2)

        @block.tensor
        def _(pe):
            run_bodies(pe, pe_window, BLOCKS // 2, False)


def ffn(nc, name, x, ident, consts, w1, b1, w2, b2, out=None, inner=None):
    with ExitStack() as ctx:
        sb = lambda n, shape, dt=F32: ctx.enter_context(nc.sbuf_tensor(f"{name}_{n}", shape, dt))
        psum = lambda n, shape: ctx.enter_context(nc.psum_tensor(f"{name}_{n}", shape, F32))
        sem = lambda n: ctx.enter_context(nc.semaphore(f"{name}_{n}"))
        LAG, GR = 3, 4
        CHUNKS = BLOCKS * FC
        norm = BlockNorm(nc, ctx, f"{name}_n", consts)
        w1r, w1h, w1l = sb("w1r", [P, EC, FF]), sb("w1h", [P, EC, FF], F32R), sb("w1l", [P, EC, FF], F32R)
        w2r, w2h, w2l = sb("w2r", [P, FC, E]), sb("w2h", [P, FC, E], F32R), sb("w2l", [P, FC, E], F32R)
        b1s, b2s = sb("b1s", [P, FC]), sb("b2s", [P, E])
        h = sb("h", [P, BT, E])
        hT = sb("hT", [P, 2, 2 * EC, BLOCK], F32R)
        g = sb("g", [P, GR, BLOCK])
        gh, gl = sb("gh", [P, GR, BLOCK], F32R), sb("gl", [P, GR, BLOCK], F32R)
        pt = psum("pt", [P, EC, BLOCK])
        pf = psum("pf", [P, 2, BLOCK])
        py = psum("py", [P, BT, BLOCK])
        s_w, s_bias, s_b = [sem("s_w1"), sem("s_w2")], sem("s_bias"), sem("s_b")
        s_whi, s_wlo = sem("s_whi"), sem("s_wlo")
        s_h, s_t, s_hi, s_lo = sem("s_h"), sem("s_t"), sem("s_hi"), sem("s_lo")
        s_f, s_g, s_gh, s_gl, s_y, s_xa = (sem(n) for n in ("s_f", "s_g", "s_gh", "s_gl", "s_y", "s_xa"))
        s_out = sem("s_out")
        xnew = sb("xnew", [P, BT, E])
        if inner is not None:
            w_down, ln_affine, scratch, ahead = inner
            norm_x, norm_h = BlockNorm(nc, ctx, f"{name}_nx", consts), BlockNorm(nc, ctx, f"{name}_nh", consts)
            xn, h2 = sb("xn", [P, BT, E]), sb("h2", [P, BT, E])
            hf = sb("hf", [P, EC, BLOCK])
            h2T, cT = sb("h2T", [P, 2 * EC, BLOCK], F32R), sb("cT", [P, 4, BLOCK], F32R)
            wdr = sb("wdr", [P, EC * 2 * P])
            wdh, wdl = sb("wdh", [P, EC, 2, P], F32R), sb("wdl", [P, EC, 2, P], F32R)
            affine = sb("affine", [P, 2 * EC])
            s_wd, s_wds = sem("s_wd"), sem("s_wds")
            s_xn, s_h2, s_t2, s_hf, s_h2hi, s_h2lo = (sem(n) for n in ("s_xn", "s_h2", "s_t2", "s_hf", "s_h2hi", "s_h2lo"))
            s_c, s_chi, s_clo = sem("s_c"), sem("s_chi"), sem("s_clo")
        s_res = sem("s_res")

        def x_tile(t, c, j):
            return tile_of(x, t * 2 * BT + c * BT + j)

        def w1_products(pe, t, c):
            f, b = c % FC, c // FC
            if f == 0:
                wait_for(pe, s_lo, t, 2 * EC, EC * (b + 1))
            wait_for(pe, s_g, t, 2 * FC, c - 1)
            cols = slice(f * P, (f + 1) * P)
            prods = [(k, w, part) for k in range(EC) for w, part in split3(w1h, w1l)]
            for i, (k, w, part) in enumerate(prods):
                mm = pe.matmul(pf[:, c % 2, :], w[:, k, cols], hT[:, b % 2, 2 * k + part, :],
                               start=i == 0, stop=i == len(prods) - 1)
            mm.then_inc(s_f, 1)

        def w2_products(pe, t, c):
            f, b = c % FC, c // FC
            if isinstance(t, int) and t == 0 and c == 0:
                pe.wait_ge(s_wlo, 4)
            wait_for(pe, s_gl, t, 2 * FC, c + 1)
            for j in range(BT):
                if f == 0:
                    wait_for(pe, s_xa, t, 2 * BT, BT * (b - 1) + j + 1)
                rows = slice(j * P, (j + 1) * P)
                for i, (a, w) in enumerate(((gh, w2h), (gh, w2l), (gl, w2h))):
                    mm = pe.matmul(py[:, j, 0:E], a[:, c % GR, rows], w[:, f, :],
                                   start=f == 0 and i == 0, stop=f == FC - 1 and i == 2)
            mm.then_inc(s_y, 1)

        def pe_window(pe, t, u):
            for s in range(FC):
                c = FC * u + s
                if live(t, 2 * FC, c, CHUNKS):
                    w1_products(pe, t, c)
                if live(t, 2 * FC, c - LAG, CHUNKS):
                    w2_products(pe, t, c - LAG)
                if s == 0 and inner is not None and live(t, 2, u - 2, BLOCKS):
                    if isinstance(t, int) and t == 1 and u == 0:
                        pe.wait_ge(s_wds, 2)
                    wait_for(pe, s_h2lo, t, 2 * EC, EC * (u - 1))
                    wait_for(pe, s_hf, t, 2 * EC, EC * (u - 1))
                    for which in range(2):
                        prods = [(k, w, part) for k in range(EC) for w, part in split3(wdh, wdl)]
                        for i, (k, w, part) in enumerate(prods):
                            mm = pe.matmul(pt[:, which, :], w[:, k, which, :], h2T[:, 2 * k + part, :],
                                           start=i == 0, stop=i == len(prods) - 1)
                        mm.then_inc(s_c, 1)
                if s == 2 and live(t, 2, u + 1, BLOCKS):
                    wait_for(pe, s_h, t, 2 * BT, BT * (u + 2))
                    if inner is not None:
                        wait_for(pe, s_clo, t, 4, 2 * (u - 1))
                    wait_for(pe, s_lo, t, 2 * EC, EC * (u + 1))
                    transpose_block(pe, pt, h, ident, s_t)
                if s == 6 and inner is not None and live(t, 2, u - 1, BLOCKS):
                    wait_for(pe, s_h2, t, 2 * BT, BT * u)
                    if live(t, 2, u + 1, BLOCKS):
                        wait_for(pe, s_lo, t, 2 * EC, EC * (u + 2))
                    else:
                        wait_for(pe, s_clo, t, 4, 2 * (u - 1))
                    transpose_block(pe, pt, h2, ident, s_t2)

        def act_window(act, t, u):
            for s in range(FC):
                c = FC * u + s
                if live(t, 2 * FC, c, CHUNKS):
                    f = c % FC
                    wait_for(act, s_f, t, 2 * FC, c + 1)
                    wait_for(act, s_gl, t, 2 * FC, c - GR + 1)
                    act.activation(g[:, c % GR, :], pf[:, c % 2, :], ACT.Gelu,
                                   bias=b1s[:, f:f + 1]).then_inc(s_g, 1)
                    wait_for(act, s_g, t, 2 * FC, c + 1)
                    wait_for(act, s_y, t, 2 * FC, c - GR + 1)
                    act.activation(gh[:, c % GR, :], g[:, c % GR, :], ACT.Copy).then_inc(s_gh, 1)
                if s == 1 and inner is not None and live(t, 2, u - 2, BLOCKS):
                    wait_for(act, s_out, t, 32, 16 * (u - 2))
                    for which in range(2):
                        wait_for(act, s_c, t, 4, 2 * (u - 2) + which + 1)
                        act.activation(cT[:, 2 * which, :], pt[:, which, :], ACT.Copy).then_inc(s_chi, 1)
                if s == 2 and live(t, 2, u + 1, BLOCKS):
                    wait_for(act, s_f, t, 2 * FC, FC * u)
                    for k in range(EC):
                        wait_for(act, s_t, t, 2 * EC, EC * (u + 1) + k + 1)
                        act.activation(hT[:, (u + 1) % 2, 2 * k, :], pt[:, k, :], ACT.Copy).then_inc(s_hi, 1)
                if s == 6 and inner is not None and live(t, 2, u - 1, BLOCKS):
                    for k in range(EC):
                        wait_for(act, s_t2, t, 2 * EC, EC * (u - 1) + k + 1)
                        wait_for(act, s_h2lo, t, 2 * EC, EC * (u - 2) + k + 1)
                        act.activation(hf[:, k, :], pt[:, k, :], ACT.Identity, bias=affine[:, EC + k:EC + k + 1],
                                       scale=affine[:, k:k + 1]).then_inc(s_hf, 1)
                    for k in range(EC):
                        wait_for(act, s_hf, t, 2 * EC, EC * (u - 1) + k + 1)
                        wait_for(act, s_c, t, 4, 2 * (u - 1))
                        act.activation(h2T[:, 2 * k, :], hf[:, k, :], ACT.Copy).then_inc(s_h2hi, 1)

        def dve_window(dve, t, u):
            for s in range(FC):
                c = FC * u + s - 1
                if live(t, 2 * FC, c, CHUNKS):
                    wait_for(dve, s_gh, t, 2 * FC, c + 1)
                    wait_for(dve, s_y, t, 2 * FC, c - GR + 1)
                    dve.tensor_tensor(gl[:, c % GR, :], g[:, c % GR, :], gh[:, c % GR, :].bitcast(F32),
                                      ALU.subtract).then_inc(s_gl, 1)
                if s == 0 and live(t, 2, u + 1, BLOCKS):
                    norm.stats(dve, t, u + 1, lambda j: x_tile(t, u + 1, j))
                if s == 1 and live(t, 2, u + 1, BLOCKS):
                    norm.shifts(dve, t, u + 1)
                    wait_for(dve, s_t, t, 2 * EC, EC * (u + 1))
                    for j in range(BT):
                        norm.apply(dve, j, h[:, j, :], x_tile(t, u + 1, j)).then_inc(s_h, 1)
                if s == 1 and inner is not None and live(t, 2, u - 2, BLOCKS):
                    for which in range(2):
                        wait_for(dve, s_chi, t, 4, 2 * (u - 2) + which + 1)
                        dve.tensor_tensor(cT[:, 2 * which + 1, :], pt[:, which, :],
                                          cT[:, 2 * which, :].bitcast(F32), ALU.subtract).then_inc(s_clo, 1)
                if s == 3 and live(t, 2, u + 1, BLOCKS):
                    for k in range(EC):
                        wait_for(dve, s_hi, t, 2 * EC, EC * (u + 1) + k + 1)
                        dve.tensor_tensor(hT[:, (u + 1) % 2, 2 * k + 1, :], pt[:, k, :],
                                          hT[:, (u + 1) % 2, 2 * k, :].bitcast(F32), ALU.subtract).then_inc(s_lo, 1)
                if s == LAG and live(t, 2, u - 1, BLOCKS):
                    wait_for(dve, s_b, t, 2, u)
                    unit = 1 if out is None else 16
                    wait_for(dve, s_res, t, 2 * unit, unit * (u - 1))
                    wait_for(dve, s_y, t, 2 * FC, FC * u)
                    for j in range(BT):
                        dve.tensor_tensor(xnew[:, j, :], x_tile(t, u - 1, j), py[:, j, 0:E],
                                          ALU.add).then_inc(s_xa, 1)
                    if inner is not None:
                        wait_for(dve, s_xa, t, 2 * BT, BT * u)
                        norm_x.stats(dve, t, u - 1, lambda j: xnew[:, j, :])
                if inner is None or not live(t, 2, u - 1, BLOCKS):
                    continue
                if s == LAG + 1:
                    norm_x.shifts(dve, t, u - 1)
                    for j in range(BT):
                        norm_x.apply(dve, j, xn[:, j, :], xnew[:, j, :]).then_inc(s_xn, 1)
                    wait_for(dve, s_xn, t, 2 * BT, BT * u)
                    norm_h.stats(dve, t, u - 1, lambda j: xn[:, j, :])
                if s == LAG + 2:
                    norm_h.shifts(dve, t, u - 1)
                    wait_for(dve, s_t2, t, 2 * EC, EC * (u - 1))
                    for j in range(BT):
                        norm_h.apply(dve, j, h2[:, j, :], xn[:, j, :]).then_inc(s_h2, 1)
                if s == 7:
                    for k in range(EC):
                        wait_for(dve, s_h2hi, t, 2 * EC, EC * (u - 1) + k + 1)
                        dve.tensor_tensor(h2T[:, 2 * k + 1, :], hf[:, k, :], h2T[:, 2 * k, :].bitcast(F32),
                                          ALU.subtract).then_inc(s_h2lo, 1)

        def pool_window(pool, t, u):
            if live(t, 2, u + 1, BLOCKS):
                norm.power(pool, t, u + 1)
                wait_for(pool, s_h, t, 2 * BT, BT * (u + 2))
                xs = tile_of(x, t * 2 * BT + (u + 1) * BT, BT).rearrange("p (a b) -> p a b", b=E)
                pool.tensor_tensor(xs, xs, b2s[:].unsqueeze(1).to_broadcast([P, BT, E]), ALU.add).then_inc(s_b, 1)
            if live(t, 2, u - 1, BLOCKS):
                dst = x[:, bass.ds(t * 2 * BT + (u - 1) * BT, BT), :]
                if inner is not None:
                    norm_x.power(pool, t, u - 1)
                    norm_h.power(pool, t, u - 1)
                    wait_for(pool, s_xn, t, 2 * BT, BT * u)
                    pool.tensor_tensor(dst, xnew[:], xn[:], ALU.add).then_inc(s_res, 1)
                elif out is None:
                    wait_for(pool, s_xa, t, 2 * BT, BT * u)
                    pool.tensor_copy(dst, xnew[:]).then_inc(s_res, 1)

        def sp_window(sp, t, u):
            if out is not None and live(t, 2, u - 1, BLOCKS):
                tiles = out.rearrange("(n p) e -> p n e", p=P)
                wait_for(sp, s_xa, t, 2 * BT, BT * u)
                sp.dma_start(tiles[:, bass.ds(t * 2 * BT + (u - 1) * BT, BT), :], xnew[:]).then_inc(s_res, 16)
            if inner is not None and live(t, 2, u - 2, BLOCKS):
                wait_for(sp, s_clo, t, 4, 2 * (u - 1))
                store_block(sp, scratch, t, u - 2, cT[:], s_out)

        block = ctx.enter_context(nc.Block())

        @block.sync
        def _(sp):
            sp.dma_start(b1s[:], b1).then_inc(s_bias, 16)
            sp.dma_start(b2s[:], b2.partition_broadcast(P)).then_inc(s_bias, 16)
            sp.dma_start(w1r[:], w1.rearrange("(c p) f -> p c f", p=P)).then_inc(s_w[0], 16)
            sp.dma_start(w2r[:], w2.rearrange("(c p) f -> p c f", p=P)).then_inc(s_w[1], 16)
            if inner is not None:
                sp.dma_start(wdr[:], w_down).then_inc(s_wd, 16)
                sp.dma_start(affine[:], ln_affine).then_inc(s_wd, 16)
            run_bodies(sp, sp_window, BLOCKS // 2, True)
            if out is not None:
                sp.wait_ge(s_res, 16 * BLOCKS)
            if inner is not None:
                sp.wait_ge(s_out, 2 * 16)
                load_ahead(sp, scratch, ahead)
                sp_window(sp, BLOCKS // 2, 1)
                sp.wait_ge(s_out, 16 * BLOCKS)

        def halves(w):
            n = w.shape[1] // 2
            return [w[:, i * n:(i + 1) * n, :].rearrange("p a b -> p (a b)") for i in range(2)]

        @block.gpsimd
        def _(pool):
            pool.wait_ge(s_bias, 32)
            pool_window(pool, -1, 1)
            if inner is not None:
                flat = lambda w: w[:].rearrange("p a b c -> p (a b c)")
                pool.wait_ge(s_wd, 32)
                pool_round(pool, flat(wdh), wdr[:], consts[0]).then_inc(s_wds, 1)
                pool.wait_ge(s_wds, 1)
                pool.tensor_tensor(flat(wdl), wdr[:], flat(wdh).bitcast(F32), ALU.subtract).then_inc(s_wds, 1)
            run_bodies(pool, pool_window, BLOCKS // 2, False)

        @block.scalar
        def _(act):
            act_window(act, -1, 1)
            for s, hi, raw in ((s_w[0], w1h, w1r), (s_w[1], w2h, w2r)):
                act.wait_ge(s, 16)
                for a, b in zip(halves(hi), halves(raw)):
                    act.activation(a, b, ACT.Copy).then_inc(s_whi, 1)
            act.wait_ge(s_bias, 32)
            if inner is not None:
                act.wait_ge(s_wd, 32)
            run_bodies(act, act_window, BLOCKS // 2, False)
            if inner is not None:
                act_window(act, BLOCKS // 2, 1)

        @block.vector
        def _(dve):
            dve_window(dve, -1, 1)
            n = 0
            for hi, lo, raw in ((w1h, w1l, w1r), (w2h, w2l, w2r)):
                for a, b, c in zip(halves(lo), halves(raw), halves(hi)):
                    n += 1
                    dve.wait_ge(s_whi, n)
                    dve.tensor_tensor(a, b, c.bitcast(F32), ALU.subtract).then_inc(s_wlo, 1)
            run_bodies(dve, dve_window, BLOCKS // 2, False)
            if inner is not None:
                dve_window(dve, BLOCKS // 2, 1)

        @block.tensor
        def _(pe):
            pe_window(pe, -1, 1)
            pe.wait_ge(s_wlo, 2)
            run_bodies(pe, pe_window, BLOCKS // 2, False)
            if inner is not None:
                pe_window(pe, BLOCKS // 2, 1)


def attention(nc, name, x, ident, zero, scratch, ahead, w_qk, w_v, w_out, scale, rope):
    with ExitStack() as ctx:
        sb = lambda n, shape, dt=F32: ctx.enter_context(nc.sbuf_tensor(f"{name}_{n}", shape, dt))
        psum = lambda n, shape: ctx.enter_context(nc.psum_tensor(f"{name}_{n}", shape, F32))
        sem = lambda n: ctx.enter_context(nc.semaphore(f"{name}_{n}"))
        WC, VC = w_qk.shape[2], w_v.shape[2]
        VW = 2 * P
        NQ = 4
        if rope is None:
            unit_steps, v_steps = {1: 0, 2: 1, 3: 2, 5: 3}, {7: 0, 9: 1, 10: 2, 11: 3}
        else:
            unit_steps, v_steps = {1: 0, 3: 1, 5: 2, 9: 3}, {11: 0, 13: 1, 14: 2, 15: 3}
            convert_steps = {5: 0, 7: 1, 9: 2, 13: 3}
        v_steps_first = {2: 0, 6: 1, 7: 2, 10: 3} if rope is not None else v_steps

        wraw, woraw = sb("wraw", [P, WC]), sb("woraw", [P, E])
        wh, wl = sb("wh", [P, 2, WC], F32R), sb("wl", [P, 2, WC], F32R)
        wvraw, wvh, wvl = sb("wvraw", [P, VC]), sb("wvh", [P, VC], F32R), sb("wvl", [P, VC], F32R)
        woh, wol = sb("woh", [P, 2, E], F32R), sb("wol", [P, 2, E], F32R)
        nat_h, nat_l = sb("nat_h", [P, 2, BLOCK], F32R), sb("nat_l", [P, 2, BLOCK], F32R)
        q_h = sb("q_h", [P, 2, 2, S], F32R)
        q_l = sb("q_l", [P, 2, 2, S], F32R)
        k_s = sb("k_s", [P, 2, 2, S], F32R)
        v = sb("v", [P, 2, KT, P])
        v_next = sb("v_next", [P, KT, P])
        p = sb("p", [P, PRING, S])
        pT = sb("pT", [P, 2, 2, KT, GW])
        nmax = sb("nmax", [P, NM])
        rsum, rinv = sb("rsum", [P, NM]), sb("rinv", [P, NM])
        o_h, o_l = sb("o_h", [P, 2, GW], F32R), sb("o_l", [P, 2, GW], F32R)
        if rope is not None:
            cos_t, sin_t = sb("cos_t", [P, S]), sb("sin_t", [P, S])
            plain, partner = sb("plain", [P, 2, BLOCK]), sb("partner", [P, 2, BLOCK])
            rot_a, rot_b, rot = sb("rot_a", [P, BLOCK]), sb("rot_b", [P, BLOCK]), sb("rot", [P, BLOCK])

        ps_s = psum("ps_s", [P, 2, S])
        ps_t = psum("ps_t", [P, 2, 4, P])
        ps_o = psum("ps_o", [P, BLOCK])
        ps_m = psum("ps_m", [P, BLOCK])

        hT, s_ht = ahead
        s_raw, s_rawo = sem("s_raw"), sem("s_rawo")
        s_rope = sem("s_rope")
        s_wsplit, s_wosplit = sem("s_wsplit"), sem("s_wosplit")
        s_proj, s_nat = sem("s_proj"), sem("s_nat")
        s_plain, s_swap = sem("s_plain"), [sem("s_swap0"), sem("s_swap1")]
        s_rot_a, s_rot_b, s_rot = sem("s_rot_a"), sem("s_rot_b"), sem("s_rot")
        s_rawv, s_wvsplit = sem("s_rawv"), sem("s_wvsplit")
        s_vp, s_v, s_vmove = sem("s_vp"), sem("s_v"), sem("s_vmove")
        s_stack = [sem("s_stack0"), sem("s_stack1")]
        s_scores, s_max, s_exp, s_tr, s_tev = (sem(n) for n in ("s_scores", "s_max", "s_exp", "s_tr", "s_tev"))
        s_recip, s_norm, s_pv, s_oh, s_ol = (sem(n) for n in ("s_recip", "s_norm", "s_pv", "s_oh", "s_ol"))
        s_wo, s_x = sem("s_wo"), sem("s_x")
        QD, KD = 8, 4
        SD = 16 * (QD + KD)

        VMOVE = 8

        def v_at(t):
            return v_steps_first if isinstance(t, int) and t < 0 else v_steps

        def users(t, u):
            for s in range(STEPS):
                c = STEPS * u + s
                if s % GS == 0:
                    g = (c - WO_LAG) // GS
                    if live(t, 2 * PG, g, NGROUP):
                        yield s, (s_x, 2 * PG, g + 1)
                elif s in unit_steps and live(t, 2, u + 1, NPAIR):
                    j = unit_steps[s]
                    if rope is not None:
                        yield s, (s_plain, 2 * NQ, NQ * (u + 1) + j + 1)
                    else:
                        yield s, (s_nat, 2 * 8, 8 * (u + 1) + 2 * j + 2)
                elif u == 1 and s in v_at(t) and live(t, 1, 1, BODIES):
                    yield s, (s_v, 8, 8 + 2 * v_at(t)[s] + 2)

        def wait_ps_m(pe, t, u, s):
            last = None
            for at, (sm, per_body, c) in users(t, u):
                if at >= s:
                    break
                last = (sm, per_body, c)
            if last is None:
                tt, uu = (t, 0) if u == 1 else (t - 1, 1)
                for at, (sm, per_body, c) in users(tt, uu):
                    last = (sm, per_body, c if u == 1 else c - per_body)
            if last is not None:
                wait_for(pe, last[0], t, last[1], last[2])

        def scores(pe, t, c):
            par, buf, cc = (c // STEPS) % 2, c % 2, c % STEPS
            head, qt = (cc % GS) // GQ, GQ * (cc // GS) + cc % GQ
            if cc == 0:
                pair = c // STEPS
                for s in s_stack:
                    wait_for(pe, s, t, 2 * SD, SD * (pair + 1))
            wait_for(pe, s_exp, t, 2 * STEPS, c - 1)
            cols = slice(qt * P, (qt + 1) * P)
            for first, q in ((True, q_h), (False, q_l)):
                for kh in range(HALVES):
                    keys = slice(kh * BLOCK, (kh + 1) * BLOCK)
                    mm = pe.matmul(ps_s[:, buf, keys], q[:, par, head, cols], k_s[:, par, head, keys],
                                   start=first, stop=not first)
            mm.then_inc(s_scores, 1)

        def transposes(pe, t, c):
            wait_for(pe, s_norm, t, 2 * STEPS, c + 1)
            for h in range(2):
                wait_for(pe, s_tev, t, 4 * STEPS, 2 * c + h - 1)
                for k in range(4):
                    kt = 4 * h + k
                    mm = pe.transpose(ps_t[:, h, k, :], p[:, c % PRING, kt * P:(kt + 1) * P], ident[:])
                mm.then_inc(s_tr, 1)

        def pv(pe, t, g, j):
            pair = g // PG
            if j == 0:
                wait_for(pe, s_tev, t, 4 * STEPS, 2 * GS * (g + 1))
                wait_for(pe, s_ol, t, 2 * PG, g)
                if pair % 2 == 0:
                    wait_for(pe, s_v, t, 8, 8 * (pair // 2 + 1))
                else:
                    wait_for(pe, s_vmove, t, 1, pair // 2 + 1)
            for kt in range(2 * j, 2 * j + 2):
                for head in (kt % 2, 1 - kt % 2):
                    rows = slice(D * head, D * (head + 1))
                    mm = pe.matmul(ps_o[rows, 0:GW], v[:, pair % 2, kt, rows], pT[:, g % 2, head, kt, :],
                                   start=kt == 0, stop=kt == KT - 1)
            if j == GS - 1:
                mm.then_inc(s_pv, 1)

        def out_project(pe, t, u, s, g):
            wait_for(pe, s_ol, t, 2 * PG, g + 1)
            wait_for(pe, s_wosplit, t, 4, 2 * (g // PG + 1))
            wait_ps_m(pe, t, u, s)
            par = (g // PG) % 2
            for qi in range(GQ):
                rows = slice(qi * P, (qi + 1) * P)
                for n, (o, w) in enumerate(((o_h, woh), (o_h, wol), (o_l, woh))):
                    mm = pe.matmul(ps_m[:, qi * E:(qi + 1) * E], o[:, g % 2, rows], w[:, par, :],
                                   start=n == 0, stop=n == 2)
            mm.then_inc(s_wo, 1)

        def project_qk(pe, t, u, s, j):
            pair = u + 1
            if j == 0:
                wait_for(pe, s_ht, t, 16, 16 * (pair // 2 + 1))
                wait_for(pe, s_wsplit, t, 4, 2 * (pair + 1))
            wait_ps_m(pe, t, u, s)
            par = pair % 2
            which, half = j // 2, j % 2
            if rope is not None:
                blocks = [(which, 2 * which)]
            else:
                blocks = [(2 * which + c, 2 * c) for c in range(EC)]
            cols = slice(half * BLOCK, (half + 1) * BLOCK)
            prods = [(wb, fb, w, f) for wb, fb in blocks for w, f in ((wh, 0), (wh, 1), (wl, 0))]
            for n, (wb, fb, w, f) in enumerate(prods):
                mm = pe.matmul(ps_m[:, :], w[:, par, wb * P:(wb + 1) * P], hT[:, fb + f, cols],
                               start=n == 0, stop=n == len(prods) - 1)
            mm.then_inc(s_proj, 1)

        def project_v(pe, t, u, s, j):
            if j == 0:
                wait_for(pe, s_wvsplit, t, 2, 2 * 2)
            wait_ps_m(pe, t, u, s)
            blocks = [(0, 2)] if rope is not None else [(c, 2 * c) for c in range(EC)]
            prods = [(wb, fb, w, f) for wb, fb in blocks for w, f in ((wvh, 0), (wvh, 1), (wvl, 0))]
            for i in range(2):
                kt = 2 * j + i
                for n, (wb, fb, w, f) in enumerate(prods):
                    mm = pe.matmul(ps_m[:, i * VW:(i + 1) * VW], hT[:, fb + f, kt * P:(kt + 1) * P],
                                   w[:, wb * VW:(wb + 1) * VW], start=n == 0, stop=n == len(prods) - 1)
            mm.then_inc(s_vp, 1)

        def pe_window(pe, t, u):
            for s in range(STEPS):
                c = STEPS * u + s
                if live(t, 2 * STEPS, c, NSTEP):
                    scores(pe, t, c)
                if live(t, 2 * STEPS, c - T_LAG, NSTEP):
                    transposes(pe, t, c - T_LAG)
                g = (c - WO_LAG) // GS
                if s % GS == 0 and live(t, 2 * PG, g, NGROUP):
                    out_project(pe, t, u, s, g)
                if s in unit_steps and live(t, 2, u + 1, NPAIR):
                    project_qk(pe, t, u, s, unit_steps[s])
                if u == 1 and s in v_at(t) and live(t, 1, 1, BODIES):
                    project_v(pe, t, u, s, v_at(t)[s])
                g, j = (c - PV_LAG) // GS, (c - PV_LAG) % GS
                if live(t, 2 * PG, g, NGROUP):
                    pv(pe, t, g, j)

        def convert(dve, t, u, jj, src):
            pair, which, half = u + 1, jj // 2, jj % 2
            wait_for(dve, s_stack[half], t, 2 * SD, SD * pair + (16 * QD if which else 0))
            mul = scale if which == 0 else 1.0
            dve.tensor_scalar(nat_h[:, half, :], src, mul, None, ALU.mult).then_inc(s_nat, 1)
            wait_for(dve, s_nat, t, 16, 8 * pair + 2 * jj + 1)
            dve.scalar_tensor_tensor(nat_l[:, half, :], src, mul, nat_h[:, half, :].bitcast(F32),
                                     ALU.mult, ALU.subtract).then_inc(s_nat, 1)

        def dve_window(dve, t, u):
            for s in range(STEPS):
                c = STEPS * u + s
                g = (c - O_LAG) // GS
                if c % GS == O_LAG % GS and live(t, 2 * PG, g, NGROUP):
                    wait_for(dve, s_oh, t, 2 * PG, g + 1)
                    dve.tensor_tensor(o_l[:, g % 2, :], ps_o[:, 0:GW], o_h[:, g % 2, :].bitcast(F32),
                                      ALU.subtract).then_inc(s_ol, 1)
                n = c - N_LAG
                if live(t, 2 * STEPS, n, NSTEP):
                    wait_for(dve, s_exp, t, 2 * STEPS, n + 1)
                    wait_for(dve, s_norm, t, 2 * STEPS, n - NM + 1)
                    dve.reciprocal(rinv[:, n % NM:n % NM + 1], rsum[:, n % NM:n % NM + 1]).then_inc(s_recip, 1)
                if live(t, 2 * STEPS, c, NSTEP):
                    wait_for(dve, s_scores, t, 2 * STEPS, c + 1)
                    dve.reduce_max(nmax[:, c % NM:c % NM + 1], ps_s[:, c % 2, :], AX_X,
                                   negate=True).then_inc(s_max, 1)
                if live(t, 2 * STEPS, n, NSTEP):
                    wait_for(dve, s_recip, t, 2 * STEPS, n + 1)
                    dve.tensor_scalar(p[:, n % PRING, :], p[:, n % PRING, :], rinv[:, n % NM:n % NM + 1], None,
                                      ALU.mult).then_inc(s_norm, 1)
                if u == 0 and s == VMOVE and live(t, 1, 0, BODIES):
                    wait_for(dve, s_pv, t, 2 * PG, 0)
                    wait_for(dve, s_v, t, 8, 8)
                    dve.tensor_copy(v[:, 1, :, :], v_next[:]).then_inc(s_vmove, 1)
                if rope is not None and s in convert_steps and live(t, 2, u + 1, NPAIR):
                    jj = convert_steps[s]
                    wait_for(dve, s_rot, t, 8, 4 * (u + 1) + jj + 1)
                    convert(dve, t, u, jj, rot[:])
                if s in unit_steps and rope is None and live(t, 2, u + 1, NPAIR):
                    wait_for(dve, s_proj, t, 2 * NQ, NQ * (u + 1) + unit_steps[s] + 1)
                    convert(dve, t, u, unit_steps[s], ps_m[:, :])
                if s - 1 in unit_steps and rope is not None and live(t, 2, u + 1, NPAIR):
                    j = unit_steps[s - 1]
                    unit, half = NQ * (u + 1) + j, j % 2
                    cols = slice(half * BLOCK, (half + 1) * BLOCK)
                    wait_for(dve, s_plain, t, 2 * NQ, unit + 1)
                    wait_for(dve, s_rot, t, 2 * NQ, unit)
                    dve.tensor_tensor(rot_a[:], plain[:, half, :], cos_t[:, cols], ALU.mult).then_inc(s_rot_a, 1)
                if u == 1 and s in v_at(t) and live(t, 1, 1, BODIES):
                    j = v_at(t)[s]
                    wait_for(dve, s_vp, t, 4, 4 + j + 1)
                    src = ps_m[:, :].rearrange("p (a b) -> p a b", b=VW)
                    wait_for(dve, s_pv, t, 2 * PG, PG)
                    dve.tensor_copy(v[:, 0, 2 * j:2 * j + 2, :], src[:, :, 0:P]).then_inc(s_v, 1)
                    wait_for(dve, s_vmove, t, 1, 1)
                    dve.tensor_copy(v_next[:, 2 * j:2 * j + 2, :], src[:, :, P:VW]).then_inc(s_v, 1)
                g = (c - WO_LAG) // GS
                if s % GS == 0 and live(t, 2 * PG, g, NGROUP):
                    wait_for(dve, s_wo, t, 2 * PG, g + 1)
                    body = t if g >= 0 else t - 1
                    tile = (body // (PAIRS // 2)) * KT + GQ * (g % PG)
                    xs = tile_of(x, tile, GQ)
                    dve.tensor_tensor(xs, xs, ps_m[:, :], ALU.add).then_inc(s_x, 1)

        def act_window(act, t, u):
            for s in range(STEPS):
                c = STEPS * u + s
                if s - 1 in unit_steps and rope is not None and live(t, 2, u + 1, NPAIR):
                    j = unit_steps[s - 1]
                    unit, half = NQ * (u + 1) + j, j % 2
                    wait_for(act, s_rot_a, t, 2 * NQ, unit - 1)
                    wait_for(act, s_rot_b, t, 2 * NQ, unit - 1)
                    wait_for(act, s_proj, t, 2 * NQ, unit + 1)
                    act.activation(plain[:, half, :], ps_m[:, :], ACT.Copy).then_inc(s_plain, 1)
                g = (c - O_LAG) // GS
                if c % GS == O_LAG % GS and live(t, 2 * PG, g, NGROUP):
                    wait_for(act, s_pv, t, 2 * PG, g + 1)
                    wait_for(act, s_wo, t, 2 * PG, g - 1)
                    act.activation(o_h[:, g % 2, :], ps_o[:, 0:GW], ACT.Copy).then_inc(s_oh, 1)
                b = c - T_LAG
                if live(t, 2 * STEPS, b, NSTEP):
                    g, head, qi = b // GS, (b % GS) // GQ, b % GQ
                    for h in range(2):
                        wait_for(act, s_tr, t, 4 * STEPS, 2 * b + h + 1)
                        if b % GS == 0 and h == 0:
                            wait_for(act, s_pv, t, 2 * PG, g - 1)
                        act.activation(pT[:, g % 2, head, 4 * h:4 * h + 4, qi * P:(qi + 1) * P],
                                       ps_t[:, h, :, :], ACT.Copy).then_inc(s_tev, 1)
                if live(t, 2 * STEPS, c, NSTEP):
                    wait_for(act, s_max, t, 2 * STEPS, c + 1)
                    wait_for(act, s_tr, t, 4 * STEPS, 2 * (c - PRING) + 2)
                    act.activation(p[:, c % PRING, :], ps_s[:, c % 2, :], ACT.Exp,
                                   bias=nmax[:, c % NM:c % NM + 1],
                                   accum_out=rsum[:, c % NM:c % NM + 1]).then_inc(s_exp, 1)

        def split_qk(pool, t, par, pair):
            wait_for(pool, s_raw, t, 32, 16 * (pair + 1))
            wait_for(pool, s_proj, t, 2 * NQ, NQ * (pair - 1))
            pool_round(pool, wh[:, par, :], wraw[:], zero).then_inc(s_wsplit, 1)
            wait_for(pool, s_wsplit, t, 4, 2 * pair + 1)
            pool.tensor_tensor(wl[:, par, :], wraw[:], wh[:, par, :].bitcast(F32),
                               ALU.subtract).then_inc(s_wsplit, 1)

        def split_v(pool, t, body):
            wait_for(pool, s_rawv, t, 16, 16 * (body + 1))
            wait_for(pool, s_vp, t, 4, 4 * body)
            pool_round(pool, wvh[:], wvraw[:], zero).then_inc(s_wvsplit, 1)
            wait_for(pool, s_wvsplit, t, 2, 2 * body + 1)
            pool.tensor_tensor(wvl[:], wvraw[:], wvh[:].bitcast(F32), ALU.subtract).then_inc(s_wvsplit, 1)

        def pool_window(pool, t, u):
            for s in range(STEPS):
                c = STEPS * u + s
                if s in unit_steps and rope is not None and live(t, 2, u + 1, NPAIR):
                    j = unit_steps[s]
                    unit, half = NQ * (u + 1) + j, j % 2
                    cols = slice(half * BLOCK, (half + 1) * BLOCK)
                    wait_for(pool, s_swap[half], t, 128, 64 * (u + 1) + 32 * (j // 2 + 1))
                    wait_for(pool, s_rot, t, 2 * NQ, unit)
                    pool.tensor_tensor(rot_b[:], partner[:, half, :], sin_t[:, cols], ALU.mult).then_inc(s_rot_b, 1)
                    wait_for(pool, s_rot_a, t, 2 * NQ, unit + 1)
                    wait_for(pool, s_rot_b, t, 2 * NQ, unit + 1)
                    wait_for(pool, s_nat, t, 16, 2 * unit)
                    pool.tensor_tensor(rot[:], rot_a[:], rot_b[:], ALU.add).then_inc(s_rot, 1)
                if s == 7 and u == 0 and live(t, 1, 1, BODIES):
                    split_v(pool, t, 1)
                if s == 3 and live(t, 2, u + 2, NPAIR):
                    split_qk(pool, t, u, u + 2)
                if s == 11 and live(t, 2, u + 1, NPAIR):
                    pair = u + 1
                    wait_for(pool, s_rawo, t, 32, 16 * (pair + 1))
                    wait_for(pool, s_wo, t, 2 * PG, PG * (pair - 1))
                    pool_round(pool, woh[:, pair % 2, :], woraw[:], zero).then_inc(s_wosplit, 1)
                    wait_for(pool, s_wosplit, t, 4, 2 * pair + 1)
                    pool.tensor_tensor(wol[:, pair % 2, :], woraw[:], woh[:, pair % 2, :].bitcast(F32),
                                       ALU.subtract).then_inc(s_wosplit, 1)

        def pair_of_batch(t, pair):
            return ((t + pair // 2) % (PAIRS // 2)) * 2 + pair % 2

        def swap(sp, t, pair, jj):
            half, unit = jj % 2, NQ * pair + jj
            wait_for(sp, s_plain, t, 2 * NQ, unit + 1)
            for row in range(2):
                sp.dma_start(partner[row::2, half, :], plain[1 - row::2, half, :]).then_inc(s_swap[half], 16)

        def stack(sp, t, pair, jj):
            par, which, half = pair % 2, jj // 2, jj % 2
            cols = slice(half * BLOCK, (half + 1) * BLOCK)
            wait_for(sp, s_nat, t, 16, 8 * pair + 2 * jj + 2)
            parts = [(q_h, nat_h, nat_h), (q_l, nat_l, nat_l)] if which == 0 else [(k_s, nat_h, nat_l)]
            for dst, top, bottom in parts:
                for head in range(2):
                    rows = slice(D * head, D * (head + 1))
                    for r, src in ((0, top), (D, bottom)):
                        sp.dma_start(dst[r:r + D, par, head, cols].bitcast(F32),
                                     src[rows, half, :].bitcast(F32)).then_inc(s_stack[half], 16)

        def reload(sp, t):
            if live(t, 1, 1, BODIES):
                source = (t + 1) // (PAIRS // 2)
                wait_for(sp, s_proj, t, 2 * NQ, 2 * NQ)
                sp.dma_start(hT[:].bitcast(F32), scratch[source].bitcast(F32)).then_inc(s_ht, 16)

        def sp_window(sp, t, u):
            if live(t, 2, u + 2, NPAIR):
                source = pair_of_batch(t, u + 2)
                wait_for(sp, s_wsplit, t, 4, 2 * (u + 2))
                sp.dma_start(wraw[:], w_qk[source]).then_inc(s_raw, 16)
            if u == 0 and live(t, 1, 1, BODIES):
                source = (t + 1) % (PAIRS // 2)
                wait_for(sp, s_wvsplit, t, 2, 2)
                sp.dma_start(wvraw[:], w_v[source]).then_inc(s_rawv, 16)
            if live(t, 2, u + 1, NPAIR):
                pair = u + 1
                source = pair_of_batch(t, pair)
                wait_for(sp, s_wosplit, t, 4, 2 * pair)
                sp.dma_start(woraw[:], w_out[source]).then_inc(s_rawo, 16)
                if rope is None:
                    for jj in range(NQ):
                        stack(sp, t, pair, jj)
                else:
                    for jj in range(NQ + 1):
                        if jj < NQ:
                            swap(sp, t, pair, jj)
                        if jj == NQ - 1 and u == 0:
                            reload(sp, t)
                        if jj > 0:
                            stack(sp, t, pair, jj - 1)
                if rope is None and u == 0:
                    reload(sp, t)

        block = ctx.enter_context(nc.Block())

        @block.sync
        def _(sp):
            sp.dma_start(wraw[:], w_qk[0]).then_inc(s_raw, 16)
            sp.dma_start(wvraw[:], w_v[0]).then_inc(s_rawv, 16)
            if rope is not None:
                sp.dma_start(cos_t[:], rope[0]).then_inc(s_rope, 16)
                sp.dma_start(sin_t[:], rope[1]).then_inc(s_rope, 16)
            run_bodies(sp, sp_window, BODIES, True)

        @block.gpsimd
        def _(pool):
            split_qk(pool, 0, 0, 0)
            split_v(pool, 0, 0)
            run_bodies(pool, pool_window, BODIES, True)

        @block.vector
        def _(dve):
            if rope is not None:
                dve.wait_ge(s_rope, 32)
            run_bodies(dve, dve_window, BODIES, True)

        @block.scalar
        def _(act):
            run_bodies(act, act_window, BODIES, True)

        @block.tensor
        def _(pe):
            run_bodies(pe, pe_window, BODIES, True)


def hybrid_stack(nc, x_in, wa_qk, wa_v, wa_out, wb_down, ln_affine, wb_qk, wb_v, wb_out, rope, w1, b1, w2, b2, out):
    feat_a = nc.dram_tensor("feat_a", [B, P, 4, S], F32R).ap()
    feat_b = nc.dram_tensor("feat_b", [B, P, 4, S], F32R).ap()
    with ExitStack() as ctx:
        feat = ctx.enter_context(nc.sbuf_tensor("feat", [P, 4, S], F32R))
        ahead_a, ahead_b = ((feat, ctx.enter_context(nc.semaphore(n))) for n in ("s_feat_a", "s_feat_b"))
        x = ctx.enter_context(nc.sbuf_tensor("x", [P, TILES, E], F32))
        ident = ctx.enter_context(nc.sbuf_tensor("ident", [P, P], F32))
        zero, eps, minus_half = (ctx.enter_context(nc.sbuf_tensor(n, [P, 1], F32))
                                 for n in ("zero", "eps", "minus_half"))
        s_id = ctx.enter_context(nc.semaphore("s_id"))
        with nc.Block() as block:
            @block.gpsimd
            def _(pool):
                pool.memset(ident[:], 0.0).then_inc(s_id, 1)
                pool.wait_ge(s_id, 1)
                pool.affine_select(out=ident[:], in_=ident[:], compare_op=ALU.not_equal, fill=1.0, base=0,
                                   pattern=[[-1, P]], channel_multiplier=1).then_inc(s_id, 1)
                for tile, value in ((zero, 0.0), (eps, EPS), (minus_half, -0.5)):
                    pool.memset(tile[:], value).then_inc(s_id, 1)
                pool.wait_ge(s_id, 5)

        consts = (zero, eps, minus_half)
        features_a(nc, x_in, x, ident, consts, feat_a, ahead_a)
        attention(nc, "a", x, ident, zero, feat_a, ahead_a, wa_qk, wa_v, wa_out, 1.0 / (D * D * H), None)
        ffn(nc, "f1", x, ident, consts, w1, b1, w2, b2, inner=(wb_down, ln_affine, feat_b, ahead_b))
        attention(nc, "b", x, ident, zero, feat_b, ahead_b, wb_qk, wb_v, wb_out, 1.0 / D ** 0.5, rope)
        ffn(nc, "f2", x, ident, consts, w1, b1, w2, b2, out=out)


def rope_tables():
    inv_freq = 1.0 / 10000.0 ** (np.arange(0, D, 2, dtype=np.float32) / D)
    freqs = np.outer(np.arange(S, dtype=np.float32), inv_freq)
    cos = np.concatenate([np.cos(freqs), np.cos(freqs)], -1)[:, ::2]
    sin = np.concatenate([np.sin(freqs), np.sin(freqs)], -1)[:, ::2]
    rows = np.arange(P)
    sign = np.where(rows % 2 == 0, -1.0, 1.0).astype(np.float32)
    pick = (rows % D) // 2
    return np.ascontiguousarray(np.stack([cos.T[pick], sin.T[pick] * sign[:, None]]).astype(np.float32))


def kernel(**inputs):
    import concourse.bacc as bacc
    from concourse.bass_utils import run_bass_kernel_spmd

    g = {k: np.asarray(v) for k, v in inputs.items()}
    ka = g["L0_attn_a_kernel"].reshape(3, PAIRS, 2, EC, P, D)
    wa_qk = ka[:2].transpose(1, 4, 0, 3, 2, 5).reshape(PAIRS, P, 2 * EC * P)
    wa_v = ka[2].reshape(PAIRS // 2, 4, EC, P, D).transpose(0, 3, 2, 1, 4).reshape(PAIRS // 2, P, EC * 2 * P)
    wa_out = g["L0_attn_a_WO"][0].reshape(D, PAIRS, 2, E).transpose(1, 2, 0, 3).reshape(PAIRS, P, E)
    up = {n: g["L0_attn_b_w_up_" + n].reshape(PAIRS, P, P) for n in "qkv"}
    wb_qk = np.stack([up["q"], up["k"]], 1).transpose(0, 3, 1, 2).reshape(PAIRS, P, 2 * P)
    wb_v = up["v"].reshape(PAIRS // 2, 2 * P, P).transpose(0, 2, 1)
    wb_out = g["L0_attn_b_w_out"].T.reshape(PAIRS, P, E)
    down = np.stack([g["L0_attn_b_w_down_q"], g["L0_attn_b_w_down_kv"]])
    wb_down = down.reshape(2, P, EC, P).transpose(3, 2, 0, 1).reshape(P, EC * 2 * P)
    ln_affine = np.stack([g["L0_attn_b_ln_scale"], g["L0_attn_b_ln_bias"]]).reshape(2 * EC, P).T
    arrays = {
        "x_in": g["L0_attn_a_x"].reshape(B * S, E), "wa_qk": wa_qk, "wa_v": wa_v, "wa_out": wa_out,
        "wb_down": wb_down, "ln_affine": ln_affine, "wb_qk": wb_qk, "wb_v": wb_v, "wb_out": wb_out,
        "rope": rope_tables(), "w1": g["L0_ffn_w1"], "b1": g["L0_ffn_b1"].reshape(FC, P).T,
        "w2": g["L0_ffn_w2"], "b2": g["L0_ffn_b2"],
    }
    arrays = {k: np.ascontiguousarray(a) for k, a in arrays.items()}
    nc = bacc.Bacc("TRN2", target_bir_lowering=False, num_devices=1)
    aps = {k: nc.dram_tensor(k, a.shape, mybir.dt.from_np(a.dtype), kind="ExternalInput").ap()
           for k, a in arrays.items()}
    out = nc.dram_tensor("out", (B * S, E), F32, kind="ExternalOutput").ap()
    hybrid_stack(nc, out=out, **aps)
    r = run_bass_kernel_spmd(nc, [arrays], core_ids=[0])
    return r.results[0]["out"].reshape(B, S, E)
```
